# Optimizing a Trainium2 kernel written in Bass

```python
import numpy as np
import jax
import jax.numpy as jnp

def _softmax(x, axis=-1):
    return jax.nn.softmax(x, axis=axis)

def _gelu(x):
    return jax.nn.gelu(x, approximate=True)

def _silu(x):
    return jax.nn.silu(x)

def _sigmoid(x):
    return jax.nn.sigmoid(x)

def _layernorm(x, axis=-1, eps=1e-05):
    m = jnp.mean(x, axis=axis, keepdims=True)
    v = jnp.var(x, axis=axis, keepdims=True)
    return (x - m) / jnp.sqrt(v + eps)

def _scatter_add(tgt, idx, src, axis=0):
    return tgt.at[idx].add(src)

def _segment_sum(src, seg, n):
    return jax.ops.segment_sum(src, seg, n)
kernel_name = 'mk_seq_postln_d1_jaxref_r8_d09523'

def setup_inputs(seed: int=0):
    np.random.seed(seed)
    _w = jnp.asarray

    def _L0_attn_setup():
        import jax, jax.numpy as jnp
        import numpy as np
        DEPTH, DIM, DFF, VOCAB = (4, 64, 256, 512)
        EPS = 1e-05

        def layernorm(x, w, b):
            mu = jnp.mean(x, axis=-1, keepdims=True)
            var = jnp.mean((x - mu) ** 2, axis=-1, keepdims=True)
            return (x - mu) * jax.lax.rsqrt(var + EPS) * w + b

        def sconv(x, phazor_c, last_conv_c):
            B, L, D = x.shape
            r = jnp.abs(phazor_c)
            p = jnp.tanh(r) * jnp.exp(1j * jnp.angle(phazor_c))
            prog = p[None, :] ** jnp.arange(L, dtype=jnp.float32)[:, None]
            filt_fft = jnp.fft.fft(prog, n=2 * L, axis=0)
            x_fft = jnp.fft.fft(x.astype(jnp.complex64), n=2 * L, axis=1)
            conv = jnp.fft.ifft(filt_fft[None] * x_fft, axis=1)[:, :L]
            conv = conv + last_conv_c[None, None, :] * prog[None] * p[None, None, :]
            return conv.real.astype(x.dtype)

        def _forward(x, Win, bin, ln1_w, ln1_b, phz_re, phz_im, lc_re, lc_im, sc_lin, ln2_w, ln2_b, W1, b1, W2, b2, lnl_w, lnl_b, Wout, bout):
            h = jnp.einsum('blv,dv->bld', x, Win) + bin

            def body(h, p):
                l1w, l1b, pr, pi, lr, li, scl, l2w, l2b, w1, b1_, w2, b2_ = p
                y = jax.nn.silu(layernorm(h, l1w, l1b))
                y = sconv(y, pr + 1j * pi, lr + 1j * li)
                h = h + y * scl
                y = layernorm(h, l2w, l2b)
                y = jax.nn.silu(jnp.einsum('bld,fd->blf', y, w1) + b1_)
                y = jnp.einsum('blf,df->bld', y, w2) + b2_
                return (h + y, None)
            xs = (ln1_w, ln1_b, phz_re, phz_im, lc_re, lc_im, sc_lin, ln2_w, ln2_b, W1, b1, W2, b2)
            h, _ = jax.lax.scan(body, h, xs)
            h = layernorm(h, lnl_w, lnl_b)
            return jnp.einsum('bld,vd->blv', h, Wout) + bout
        key = jax.random.key(seed)
        ks = jax.random.split(key, 20)
        f32 = jnp.float32
        inp = {}
        inp['x'] = jax.random.normal(ks[0], (2, 512, VOCAB), dtype=f32)
        inp['Win'] = jax.random.normal(ks[1], (DIM, VOCAB), dtype=f32) * VOCAB ** (-0.5)
        inp['bin'] = jnp.zeros((DIM,), f32)
        inp['ln1_w'] = jnp.ones((DEPTH, DIM), f32)
        inp['ln1_b'] = jnp.zeros((DEPTH, DIM), f32)
        ang = 2 * np.pi * jnp.arange(DIM, dtype=f32) / DIM
        mag = jnp.abs(jax.random.normal(ks[2], (DEPTH, DIM), dtype=f32))
        inp['phz_re'] = mag * jnp.cos(ang)[None]
        inp['phz_im'] = mag * jnp.sin(ang)[None]
        inp['lc_re'] = jax.random.normal(ks[3], (DEPTH, DIM), dtype=f32)
        inp['lc_im'] = jax.random.normal(ks[4], (DEPTH, DIM), dtype=f32)
        inp['sc_lin'] = jnp.ones((DEPTH, DIM), f32)
        inp['ln2_w'] = jnp.ones((DEPTH, DIM), f32)
        inp['ln2_b'] = jnp.zeros((DEPTH, DIM), f32)
        inp['W1'] = jax.random.normal(ks[5], (DEPTH, DFF, DIM), dtype=f32) * DIM ** (-0.5)
        inp['b1'] = jnp.zeros((DEPTH, DFF), f32)
        inp['W2'] = jax.random.normal(ks[6], (DEPTH, DIM, DFF), dtype=f32) * DFF ** (-0.5)
        inp['b2'] = jnp.zeros((DEPTH, DIM), f32)
        inp['lnl_w'] = jnp.ones((DIM,), f32)
        inp['lnl_b'] = jnp.zeros((DIM,), f32)
        inp['Wout'] = jax.random.normal(ks[7], (VOCAB, DIM), dtype=f32) * DIM ** (-0.5)
        inp['bout'] = jnp.zeros((VOCAB,), f32)
        return inp
    _L0_attn_in = _L0_attn_setup()

    def _L0_ffn_setup():
        import jax, jax.numpy as jnp
        import numpy as np
        H = 512
        I = 1376
        CS = 8
        CB = 8192

        def _dequant(codebook, idx):
            return codebook[idx].reshape(idx.shape[0], -1)
        key = jax.random.key(seed)
        k0, k1, k2, k3, k4 = jax.random.split(key, 5)
        x = jax.random.normal(k0, (4, 256, H), dtype=jnp.float32)
        codebook = jax.random.normal(k1, (CB, CS), dtype=jnp.float32)
        idx_gate = jax.random.randint(k2, (I, H // CS), 0, CB, dtype=jnp.int32)
        idx_up = jax.random.randint(k3, (I, H // CS), 0, CB, dtype=jnp.int32)
        idx_down = jax.random.randint(k4, (H, I // CS), 0, CB, dtype=jnp.int32)
        return {'x': x, 'codebook': codebook, 'idx_gate': idx_gate, 'idx_up': idx_up, 'idx_down': idx_down}
    _L0_ffn_in = _L0_ffn_setup()
    _d = {'L0_attn_x': _L0_attn_in['x'], 'L0_attn_Win': _L0_attn_in['Win'], 'L0_attn_bin': _L0_attn_in['bin'], 'L0_attn_ln1_w': _L0_attn_in['ln1_w'], 'L0_attn_ln1_b': _L0_attn_in['ln1_b'], 'L0_attn_phz_re': _L0_attn_in['phz_re'], 'L0_attn_phz_im': _L0_attn_in['phz_im'], 'L0_attn_lc_re': _L0_attn_in['lc_re'], 'L0_attn_lc_im': _L0_attn_in['lc_im'], 'L0_attn_sc_lin': _L0_attn_in['sc_lin'], 'L0_attn_ln2_w': _L0_attn_in['ln2_w'], 'L0_attn_ln2_b': _L0_attn_in['ln2_b'], 'L0_attn_W1': _L0_attn_in['W1'], 'L0_attn_b1': _L0_attn_in['b1'], 'L0_attn_W2': _L0_attn_in['W2'], 'L0_attn_b2': _L0_attn_in['b2'], 'L0_attn_lnl_w': _L0_attn_in['lnl_w'], 'L0_attn_lnl_b': _L0_attn_in['lnl_b'], 'L0_attn_Wout': _L0_attn_in['Wout'], 'L0_attn_bout': _L0_attn_in['bout'], 'L0_ffn_codebook': _L0_ffn_in['codebook'], 'L0_ffn_idx_gate': _L0_ffn_in['idx_gate'], 'L0_ffn_idx_up': _L0_ffn_in['idx_up'], 'L0_ffn_idx_down': _L0_ffn_in['idx_down']}
    _x0 = _d['L0_attn_x']
    _d['L0_attn_x'] = jax.random.normal(jax.random.fold_in(jax.random.key(seed), 1), (1, 2048, 512), dtype=_x0.dtype)
    del _x0
    return _d

def reference(L0_attn_x, L0_attn_Win, L0_attn_bin, L0_attn_ln1_w, L0_attn_ln1_b, L0_attn_phz_re, L0_attn_phz_im, L0_attn_lc_re, L0_attn_lc_im, L0_attn_sc_lin, L0_attn_ln2_w, L0_attn_ln2_b, L0_attn_W1, L0_attn_b1, L0_attn_W2, L0_attn_b2, L0_attn_lnl_w, L0_attn_lnl_b, L0_attn_Wout, L0_attn_bout, L0_ffn_codebook, L0_ffn_idx_gate, L0_ffn_idx_up, L0_ffn_idx_down):

    def _L0_attn_ref(x, Win, bin, ln1_w, ln1_b, phz_re, phz_im, lc_re, lc_im, sc_lin, ln2_w, ln2_b, W1, b1, W2, b2, lnl_w, lnl_b, Wout, bout):
        import jax, jax.numpy as jnp
        import numpy as np
        DEPTH, DIM, DFF, VOCAB = (4, 64, 256, 512)
        EPS = 1e-05

        def layernorm(x, w, b):
            mu = jnp.mean(x, axis=-1, keepdims=True)
            var = jnp.mean((x - mu) ** 2, axis=-1, keepdims=True)
            return (x - mu) * jax.lax.rsqrt(var + EPS) * w + b

        def sconv(x, phazor_c, last_conv_c):
            B, L, D = x.shape
            r = jnp.abs(phazor_c)
            p = jnp.tanh(r) * jnp.exp(1j * jnp.angle(phazor_c))
            prog = p[None, :] ** jnp.arange(L, dtype=jnp.float32)[:, None]
            filt_fft = jnp.fft.fft(prog, n=2 * L, axis=0)
            x_fft = jnp.fft.fft(x.astype(jnp.complex64), n=2 * L, axis=1)
            conv = jnp.fft.ifft(filt_fft[None] * x_fft, axis=1)[:, :L]
            conv = conv + last_conv_c[None, None, :] * prog[None] * p[None, None, :]
            return conv.real.astype(x.dtype)

        def _forward(x, Win, bin, ln1_w, ln1_b, phz_re, phz_im, lc_re, lc_im, sc_lin, ln2_w, ln2_b, W1, b1, W2, b2, lnl_w, lnl_b, Wout, bout):
            h = jnp.einsum('blv,dv->bld', x, Win) + bin

            def body(h, p):
                l1w, l1b, pr, pi, lr, li, scl, l2w, l2b, w1, b1_, w2, b2_ = p
                y = jax.nn.silu(layernorm(h, l1w, l1b))
                y = sconv(y, pr + 1j * pi, lr + 1j * li)
                h = h + y * scl
                y = layernorm(h, l2w, l2b)
                y = jax.nn.silu(jnp.einsum('bld,fd->blf', y, w1) + b1_)
                y = jnp.einsum('blf,df->bld', y, w2) + b2_
                return (h + y, None)
            xs = (ln1_w, ln1_b, phz_re, phz_im, lc_re, lc_im, sc_lin, ln2_w, ln2_b, W1, b1, W2, b2)
            h, _ = jax.lax.scan(body, h, xs)
            h = layernorm(h, lnl_w, lnl_b)
            return jnp.einsum('bld,vd->blv', h, Wout) + bout
        return _forward(x, Win, bin, ln1_w, ln1_b, phz_re, phz_im, lc_re, lc_im, sc_lin, ln2_w, ln2_b, W1, b1, W2, b2, lnl_w, lnl_b, Wout, bout)

    def _L0_ffn_ref(x, codebook, idx_gate, idx_up, idx_down):
        import jax, jax.numpy as jnp
        import numpy as np
        H = 512
        I = 1376
        CS = 8
        CB = 8192

        def _dequant(codebook, idx):
            return codebook[idx].reshape(idx.shape[0], -1)
        Wg = _dequant(codebook, idx_gate)
        Wu = _dequant(codebook, idx_up)
        Wd = _dequant(codebook, idx_down)
        g = jnp.einsum('bsh,ih->bsi', x, Wg)
        u = jnp.einsum('bsh,ih->bsi', x, Wu)
        h = jax.nn.silu(g) * u
        return jnp.einsum('bsi,hi->bsh', h, Wd)
    x = L0_attn_x
    x = _layernorm(x + _L0_attn_ref(x, L0_attn_Win, L0_attn_bin, L0_attn_ln1_w, L0_attn_ln1_b, L0_attn_phz_re, L0_attn_phz_im, L0_attn_lc_re, L0_attn_lc_im, L0_attn_sc_lin, L0_attn_ln2_w, L0_attn_ln2_b, L0_attn_W1, L0_attn_b1, L0_attn_W2, L0_attn_b2, L0_attn_lnl_w, L0_attn_lnl_b, L0_attn_Wout, L0_attn_bout), axis=-1)
    x = _layernorm(x + _L0_ffn_ref(x, L0_ffn_codebook, L0_ffn_idx_gate, L0_ffn_idx_up, L0_ffn_idx_down), axis=-1)
    return x

_drawn_inputs = setup_inputs


def setup_inputs(seed=0):
    import zlib

    import numpy as np

    out = dict(_drawn_inputs(seed))
    spreads = {'L0_attn_bin': (0.0, 0.1),
     'L0_attn_ln1_w': (1.0, 0.2),
     'L0_attn_ln1_b': (0.0, 0.1),
     'L0_attn_sc_lin': (1.0, 0.2),
     'L0_attn_ln2_w': (1.0, 0.2),
     'L0_attn_ln2_b': (0.0, 0.1),
     'L0_attn_b1': (0.0, 0.1),
     'L0_attn_b2': (0.0, 0.1),
     'L0_attn_lnl_w': (1.0, 0.2),
     'L0_attn_lnl_b': (0.0, 0.1),
     'L0_attn_bout': (0.0, 0.1)}
    factors = {'L0_attn_lc_re': 6.355, 'L0_attn_lc_im': 4.905}
    for name, (base, spread) in spreads.items():
        noise = np.random.default_rng([zlib.crc32(name.encode()), seed]).standard_normal(out[name].shape)
        drawn = base * np.exp(spread * noise) if base else spread * noise
        out[name] = jnp.asarray(drawn.astype(out[name].dtype))
    for name, factor in factors.items():
        out[name] = (out[name] * factor).astype(out[name].dtype)
    return out
```

```python
from contextlib import ExitStack

import numpy as np
import concourse.bass as bass
from concourse import mybir

F32 = mybir.dt.float32
F32R = mybir.dt.float32r
I32 = mybir.dt.int32
ALU = mybir.AluOpType
ACT = mybir.ActivationFunctionType

P = 128
EPS = 1e-5
TINY = 1e-30

LN1_W, LN1_B, SC_LIN, LN2_W, LN2_B, B2, PHZ_RE, PHZ_IM, LC_RE, LC_IM, B1 = range(11)
PER_LAYER = 12
COS_C, SIN_C, DECAY, STATE0, B1P = 12, 13, 14, 15, 16
LAYER_COLS = 18


def build(nc, a, out):
    L, D = a["L0_attn_ln1_w"].shape
    T, V = a["L0_attn_x"].shape[1:]
    FF = a["L0_attn_W1"].shape[1]
    CB, CS = a["L0_ffn_codebook"].shape
    INNER = a["L0_ffn_idx_gate"].shape[0]
    C = 512
    NC = T // C
    NT = T // P
    TPC = C // P
    KT = V // P
    FK = FF // P
    FULL = INNER // P
    REST = INNER - FULL * P
    JG = V // CS
    JD = P // CS
    NL = L * PER_LAYER
    LNL_W, LNL_B, BIN, ROWS = NL, NL + 1, NL + 2, NL + 3

    x_in = a["L0_attn_x"][0].rearrange("(t p) v -> p t v", p=P)
    y_out = out[0].rearrange("(t p) v -> p t v", p=P)

    ctx = ExitStack()
    attn_ctx = ExitStack()
    with ctx:
        def sb(name, shape, dt=F32, where=ctx):
            return where.enter_context(nc.sbuf_tensor(name, shape, dt))

        def sem(name):
            return ctx.enter_context(nc.semaphore(name))

        bank = [ctx.enter_context(nc.psum_tensor(f"bank{i}", [P, 512], F32)) for i in range(8)]

        x = sb("x", [P, NT, V])
        x1t_hi = sb("x1t_hi", [P, KT, T], F32R)
        ident = sb("ident", [P, P])
        stage_gate = [sb(f"stage_gate{b}", [P, V]) for b in range(2)]
        stage_up = [sb(f"stage_up{b}", [P, V]) for b in range(2)]
        stage_down = [sb(f"stage_down{b}", [P, KT, P]) for b in range(2)]
        idx_gate = [sb(f"idx_gate{b}", [P, JG], I32) for b in range(2)]
        idx_up = [sb(f"idx_up{b}", [P, JG], I32) for b in range(2)]
        idx_down = [sb(f"idx_down{b}", [P, KT, JD], I32) for b in range(2)]
        stats = sb("stats", [P, NT, 6])
        mv = sb("mv", [P, NT, 2])
        rstd = sb("rstd", [P, NT])
        eps = sb("eps", [P, 1])
        hn = sb("hn", [D + 1, T])
        woutt = sb("woutt", [D + 1, V])

        with attn_ctx:
            def at(name, shape, dt=F32):
                return sb(name, shape, dt, attn_ctx)

            h = at("h", [D, T])
            sq = at("sq", [P, NC, C])
            rs = at("rs", [P, NC, C])
            xn = at("xn", [P, NC, C])
            g = at("g", [P, NC, C])
            ff = at("ff", [P, NC, FK, C])
            rows = at("rows", [ROWS, P])
            cols = at("cols", [P, L, LAYER_COLS])
            last_cols = at("last_cols", [P, 3])
            lay = at("lay", [P, LAYER_COLS])
            tab = at("tab", [P, L, C])
            tab_l = at("tab_l", [P, C])
            cosp = at("cosp", [P, L, 10])
            sinp = at("sinp", [P, L, 10])
            small = at("small", [P, 12, L])
            sgn = at("sgn", [P, 1])
            perm = at("perm", [P, P])
            dup_ident = at("dup_ident", [P, D])
            centre = at("centre", [D, P])
            mean_p = at("mean_p", [P, P])
            mean_d = at("mean_d", [D, P])
            turn = at("turn", [P, P])
            turn_a = at("turn_a", [P, P])
            scale_add = at("scale_add", [P, D])
            w1_in = at("w1_in", [P, L * FK, D])
            w2_in = at("w2_in", [D, L, FF])
            win_in = at("win_in", [D, V])
            wout_in = at("wout_in", [P, KT, D])
            w1t_all = at("w1t_all", [D, L, FF])
            w2t_all = at("w2t_all", [P, L, FK, D])
            w1t = at("w1t", [D, FF])
            w2t = at("w2t", [P, FK, D])
            wint = at("wint", [P, KT, D])
            bout_row = at("bout_row", [1, V])

        xt, tabq, tmp = ff, g, xn

        x1t_lo = sb("x1t_lo", [P, KT, T], F32R)
        wg = [[sb(f"wg{b}{p}", [P, KT, P], F32R) for p in range(2)] for b in range(2)]
        wu = [[sb(f"wu{b}{p}", [P, KT, P], F32R) for p in range(2)] for b in range(2)]
        wd = [[sb(f"wd{b}{p}", [P, V], F32R) for p in range(2)] for b in range(2)]
        silu = sb("silu", [P, 2, C])
        prod = sb("prod", [P, 2, C])
        act_hi = sb("act_hi", [P, T], F32R)
        act_lo = sb("act_lo", [P, T], F32R)

        sem_names = """idx_rows_in0 idx_rows_in1 gate_in0 gate_in1 up_in0 up_in1 down_in0 down_in1
            x_in0 x_in1 x_in2 x_in3 rows_in w_in bout_in consts_made masks_made turned_w turned_x x_kept h_made bout_made
            cols_made phase_sqrt phase_tanh q_made mag_made link b1_sum b1_made tables_made layer_cols w_copied
            centred squared averaged rooted normed silu_made rotated scanned damped mixed h_mid normed2
            spread ff_made ff_back last_normed attn_out x_added aggregated rstd_made x1_made x1_turned x1_hi x1_lo
            stage_free turned_stage w_hi w_lo gate_made up_made gate_silu product act_hi_made act_lo_made
            down_made down_added out_normed stored h_sum w_kept eps_made means_made bout_sum
            stage_claimed lay_kept turn_begun turned_back stats_made""".split()
        s = {n: sem(n) for n in sem_names}

        ROW_DMAS = 2 * 10 + FK + 2 * 3
        block = ctx.enter_context(nc.Block())

        @block.sync
        def _(sp):
            def index_rows(b, waited, gate, up, down):
                if waited is not None:
                    sp.wait_ge(s[f"gate_in{b}"], waited)
                    sp.wait_ge(s[f"up_in{b}"], waited)
                    sp.wait_ge(s[f"down_in{b}"], waited)
                n, j = gate.shape[0], down.shape[2]
                sp.dma_start(idx_gate[b][0:n, :], gate).then_inc(s[f"idx_rows_in{b}"], 16)
                sp.dma_start(idx_up[b][0:n, :], up).then_inc(s[f"idx_rows_in{b}"], 16)
                sp.dma_start(idx_down[b][:, :, 0:j], down).then_inc(s[f"idx_rows_in{b}"], 16)

            ig, iu = a["L0_ffn_idx_gate"], a["L0_ffn_idx_up"]
            idn = a["L0_ffn_idx_down"].rearrange("(q p) j -> p q j", p=P)

            def tile_indices(b, k, waited):
                index_rows(b, waited, ig[bass.ds(k * P, P), :], iu[bass.ds(k * P, P), :], idn[:, :, bass.ds(k * JD, JD)])

            tile_indices(0, 0, None)
            tile_indices(1, 1, None)
            per_layer = ["L0_attn_ln1_w", "L0_attn_ln1_b", "L0_attn_sc_lin", "L0_attn_ln2_w", "L0_attn_ln2_b", "L0_attn_b2",
                         "L0_attn_phz_re", "L0_attn_phz_im", "L0_attn_lc_re", "L0_attn_lc_im"]
            for n, name in enumerate(per_layer):
                for half in range(2):
                    sp.dma_start(rows[n:NL:PER_LAYER, half * D:(half + 1) * D], a[name]).then_inc(s["rows_in"], 16)
            for k in range(FK):
                sp.dma_start(rows[B1 + k:NL:PER_LAYER, :], a["L0_attn_b1"][:, k * P:(k + 1) * P]).then_inc(s["rows_in"], 16)
            for n, name in ((LNL_W, "L0_attn_lnl_w"), (LNL_B, "L0_attn_lnl_b"), (BIN, "L0_attn_bin")):
                for half in range(2):
                    sp.dma_start(rows[n:n + 1, half * D:(half + 1) * D], a[name].rearrange("(o d) -> o d", o=1)).then_inc(s["rows_in"], 16)
            with sp.Fori(1, FULL // 2) as i:
                for b in range(2):
                    tile_indices(b, 2 * i + b, i * (16 * JG))
            last = FULL * P
            index_rows(0, (FULL // 2) * 16 * JG, ig[last:INNER, :], iu[last:INNER, :], idn[:, :, FULL * JD:])
            for t in range(NT):
                sp.wait_ge(s["out_normed"], t + 1)
                sp.dma_start(y_out[:, t, :], x[:, t, :]).then_inc(s["stored"], 16)
            sp.wait_ge(s["stored"], 16 * NT)

        @block.gpsimd
        def _(pool):
            pool.memset(ident[:, :], 0.0).then_inc(s["consts_made"], 1)
            pool.memset(perm[:, :], 0.0).then_inc(s["consts_made"], 1)
            pool.memset(dup_ident[:, :], 0.0).then_inc(s["consts_made"], 1)
            pool.wait_ge(s["consts_made"], 3)
            pool.affine_select(out=ident[:, :], in_=ident[:, :], compare_op=ALU.not_equal, fill=1.0, base=0,
                               pattern=[[-1, P]], channel_multiplier=1).then_inc(s["masks_made"], 1)
            for base, m in ((-D, perm), (D, perm), (0, dup_ident), (-D, dup_ident)):
                if base == D or (base == -D and m is dup_ident):
                    pool.wait_ge(s["masks_made"], 2 if m is perm else 4)
                pool.affine_select(out=m[:, :], in_=m[:, :], compare_op=ALU.not_equal, fill=1.0, base=base,
                                   pattern=[[-1, m.shape[1]]], channel_multiplier=1).then_inc(s["masks_made"], 1)
            pool.sem_inc(s["stage_free"], 6)

            def gather(dst, idx, sm):
                pool.indirect_dma_start(dst, None, a["L0_ffn_codebook"],
                                        bass.IndirectOffsetOnAxis(ap=idx, axis=0)).then_inc(sm, 16)

            def gathers(b, arrived, freed, n, jd):
                pool.wait_ge(s[f"idx_rows_in{b}"], arrived)
                for m, (stage, idx, sm) in enumerate(((stage_gate, idx_gate, "gate_in"), (stage_up, idx_up, "up_in"))):
                    pool.wait_ge(s["stage_free"], freed + m + 1)
                    pool.sem_inc(s["stage_claimed"], 1)
                    for j in range(JG):
                        gather(stage[b][0:n, j * CS:(j + 1) * CS], idx[b][0:n, j:j + 1], s[f"{sm}{b}"])
                pool.wait_ge(s["stage_free"], freed + 3)
                pool.sem_inc(s["stage_claimed"], 1)
                for q in range(KT):
                    for j in range(jd):
                        gather(stage_down[b][:, q, j * CS:(j + 1) * CS], idx_down[b][:, q, j:j + 1], s[f"down_in{b}"])

            with pool.Fori(0, FULL // 2) as i:
                for b in range(2):
                    gathers(b, i * 48 + 48, i * 6 + 3 * b, P, JD)
            gathers(0, (FULL // 2) * 48 + 48, 3 * FULL, REST, REST // CS)

        @block.scalar
        def _(act):
            for c in range(NC):
                act.dma_start(x[:, c * TPC:(c + 1) * TPC, :], x_in[:, c * TPC:(c + 1) * TPC, :]).then_inc(s[f"x_in{c}"], 16)
            act.dma_start(win_in[:, :], a["L0_attn_Win"]).then_inc(s["w_in"], 16)
            act.dma_start(w1_in[:, :, :], a["L0_attn_W1"].rearrange("l (k p) d -> p (l k) d", p=P)).then_inc(s["w_in"], 16)
            act.dma_start(w2_in[:, :, :], a["L0_attn_W2"].rearrange("l d f -> d l f")).then_inc(s["w_in"], 16)
            act.dma_start(wout_in[:, :, :], a["L0_attn_Wout"].rearrange("(k p) d -> p k d", p=P)).then_inc(s["w_in"], 16)
            act.dma_start(bout_row[:, :], a["L0_attn_bout"].rearrange("(o v) -> o v", o=1)).then_inc(s["bout_in"], 16)

            def keep_x(t):
                act.wait_ge(s["turned_x"], t + 1)
                c = t // TPC
                if c >= 2:
                    act.wait_ge(s["h_sum"], c - 1)
                act.activation(xt[:, c % 2 * 2:c % 2 * 2 + 2, :, (t % TPC) * P:(t % TPC + 1) * P],
                               bank[4 + t % 4][:, :].rearrange("p (a b n) -> p a b n", a=2, b=2), ACT.Copy).then_inc(s["x_kept"], 1)

            def keep_h(c):
                act.wait_ge(s["h_sum"], c + 1)
                act.activation(h[:, c * C:(c + 1) * C], bank[c][0:D, :], ACT.Identity, bias=last_cols[0:D, 2:3]).then_inc(s["h_made"], 1)

            for t in range(TPC):
                keep_x(t)
            act.wait_ge(s["q_made"], 1)
            act.activation(small[:, 8, :], small[:, 7, :], ACT.Sqrt).then_inc(s["phase_sqrt"], 1)
            for t in range(TPC, 2 * TPC):
                keep_x(t)
            act.wait_ge(s["mag_made"], 1)
            act.activation(cols[:, :, DECAY], small[:, 9, :], ACT.Tanh).then_inc(s["phase_tanh"], 1)
            act.wait_ge(s["cols_made"], 1)
            keep_h(0)
            for c in range(2, NC):
                for t in range(c * TPC, (c + 1) * TPC):
                    keep_x(t)
                keep_h(c - 1)
            keep_h(NC - 1)

            def root(dst, src):
                return act.activation(dst, src, ACT.Abs_reciprocal_sqrt, bias=eps[0:dst.shape[0], :])

            act.wait_ge(s["eps_made"], 1)
            with act.Fori(0, L) as l:
                act.wait_ge(s["h_made"], l * NC + NC)
                act.wait_ge(s["w_kept"], 5)
                act.activation(w1t[:, :], w1t_all[:, bass.ds(l, 1), :].rearrange("d o f -> d (o f)"), ACT.Copy).then_inc(s["w_copied"], 1)
                act.activation(w2t[:, :, :].rearrange("p k d -> p (k d)"),
                               w2t_all[:, bass.ds(l, 1), :, :].rearrange("p o k d -> p (o k d)"), ACT.Copy).then_inc(s["w_copied"], 1)
                for c in range(NC):
                    act.wait_ge(s["centred"], l * 2 * NC + c + 1)
                    act.activation(sq[:, c, :], bank[c][:, :], ACT.Square).then_inc(s["squared"], 1)
                for c in range(NC):
                    act.wait_ge(s["averaged"], l * 2 * NC + c + 1)
                    root(rs[:, c, :], bank[4 + c][:, :]).then_inc(s["rooted"], 1)
                act.wait_ge(s["layer_cols"], l + 1)
                for c in range(NC):
                    act.wait_ge(s["normed"], l * NC + c + 1)
                    act.activation(sq[:, c, :], xn[:, c, :], ACT.Silu, bias=lay[:, LN1_B:LN1_B + 1],
                                   scale=lay[:, LN1_W:LN1_W + 1]).then_inc(s["silu_made"], 1)
                for c in range(NC):
                    act.wait_ge(s["centred"], l * 2 * NC + NC + c + 1)
                    act.activation(sq[0:D, c, :], bank[4 + c][0:D, :], ACT.Square).then_inc(s["squared"], 1)
                for c in range(NC):
                    act.wait_ge(s["averaged"], l * 2 * NC + NC + c + 1)
                    root(rs[0:D, c, :], bank[c][0:D, :]).then_inc(s["rooted"], 1)
                for c in range(NC):
                    act.wait_ge(s["spread"], l * NC + c + 1)
                    for k in range(FK):
                        last = act.activation(ff[:, c, k, :], bank[4 * k + c][:, :], ACT.Silu, bias=lay[:, B1P + k:B1P + k + 1])
                    last.then_inc(s["ff_made"], 1)
            for c in range(NC):
                act.wait_ge(s["centred"], L * 2 * NC + c + 1)
                act.activation(sq[0:D, c, :], bank[c][0:D, :], ACT.Square).then_inc(s["squared"], 1)
            for c in range(NC):
                act.wait_ge(s["averaged"], L * 2 * NC + c + 1)
                root(rs[0:D, c, :], bank[4 + c][0:D, :]).then_inc(s["rooted"], 1)

            def keep_x1(t):
                act.wait_ge(s["x1_turned"], t + 1)
                act.activation(x1t_hi[:, :, t * P:(t + 1) * P], bank[4 + t % 4][:, :].rearrange("p (k n) -> p k n", k=KT),
                               ACT.Copy).then_inc(s["x1_hi"], 1)

            for t in range(NT + 2):
                if t < NT:
                    act.wait_ge(s["aggregated"], t + 1)
                    root(rstd[:, t:t + 1], mv[:, t, 1:2]).then_inc(s["rstd_made"], 1)
                if t >= 2:
                    keep_x1(t - 2)

            def ffn(b, k, n):
                for m, w in enumerate((wg, wu)):
                    act.wait_ge(s["turned_stage"], 3 * k + m + 1)
                    act.activation(w[b][0][:, :, 0:n], bank[2 + m][:, :].rearrange("p (k n) -> p k n", k=KT)[:, :, 0:n],
                                   ACT.Copy).then_inc(s["w_hi"], 1)
                act.wait_ge(s["turned_stage"], 3 * k + 3)
                act.activation(wd[b][0][0:n, :], bank[4][0:n, :], ACT.Copy).then_inc(s["w_hi"], 1)
                for c in range(NC + 1):
                    if c < NC:
                        act.wait_ge(s["gate_made"], NC * k + c + 1)
                        if c >= 2:
                            act.wait_ge(s["product"], NC * k + c - 1)
                        act.activation(silu[0:n, c % 2, :], bank[0][0:n, :], ACT.Silu).then_inc(s["gate_silu"], 1)
                    if c:
                        act.wait_ge(s["product"], NC * k + c)
                        act.activation(act_hi[0:n, (c - 1) * C:c * C], prod[0:n, (c - 1) % 2, :], ACT.Copy).then_inc(s["act_hi_made"], 1)

            with act.Fori(0, FULL // 2) as i:
                for b in range(2):
                    ffn(b, 2 * i + b, P)
            ffn(0, FULL, REST)
            for t in range(NT):
                act.wait_ge(s["aggregated"], NT + t + 1)
                root(rstd[:, t:t + 1], mv[:, t, 1:2]).then_inc(s["rstd_made"], 1)

        @block.tensor
        def _(pe):
            def mm(dst, lhs, rhs, start=True, stop=True):
                return pe.matmul(dst, lhs, rhs, start=start, stop=stop)

            pe.wait_ge(s["masks_made"], 1)
            pe.wait_ge(s["rows_in"], 16 * ROW_DMAS)
            pe.transpose(bank[0][:, 0:ROWS], rows[:, :], ident[0:ROWS, 0:ROWS]).then_inc(s["turned_w"], 1)

            def turn_x(t):
                if t % TPC == 0:
                    pe.wait_ge(s[f"x_in{t // TPC}"], 16)
                if t >= 4:
                    pe.wait_ge(s["x_kept"], t - 3)
                for k in range(KT):
                    last = pe.transpose(bank[4 + t % 4][:, k * P:(k + 1) * P], x[:, t, k * P:(k + 1) * P], ident[:, :])
                last.then_inc(s["turned_x"], 1)

            def h_in(c):
                pe.wait_ge(s["x_kept"], (c + 1) * TPC)
                if c == 0:
                    pe.wait_ge(s["w_kept"], 5)
                    pe.wait_ge(s["b1_made"], 1)
                for k in range(KT):
                    last = mm(bank[c][0:D, :], wint[:, k, :], xt[:, c % 2 * 2 + k // 2, k % 2, :], k == 0, k == KT - 1)
                last.then_inc(s["h_sum"], 1)

            for t in range(TPC):
                turn_x(t)
            pe.wait_ge(s["w_in"], 64)
            for half in range(2):
                for n in range(4):
                    m = half * 4 + n
                    last = pe.transpose(bank[1 + half][0:D, n * P:(n + 1) * P], w1_in[:, m, :], ident[:, :])
                last.then_inc(s["turned_w"], 1)
            for m in range(L * FK):
                last = pe.transpose(bank[3][:, m * D:(m + 1) * D], w2_in[:, m // FK, (m % FK) * P:(m % FK + 1) * P], ident[0:D, 0:D])
            last.then_inc(s["turned_w"], 1)
            pe.wait_ge(s["w_kept"], 2)
            for k in range(KT):
                last = pe.transpose(bank[1][:, k * D:(k + 1) * D], win_in[:, k * P:(k + 1) * P], ident[0:D, 0:D])
            last.then_inc(s["turned_w"], 1)
            for k in range(KT):
                last = pe.transpose(bank[2][0:D, k * P:(k + 1) * P], wout_in[:, k, :], ident[:, :])
            last.then_inc(s["turned_w"], 1)
            for t in range(TPC, 2 * TPC):
                turn_x(t)
            pe.wait_ge(s["cols_made"], 1)
            pe.wait_ge(s["w_kept"], 5)
            for m in range(L * FK):
                last = mm(bank[0][:, m:m + 1], w1t_all[:, m // FK, (m % FK) * P:(m % FK + 1) * P], cols[0:D, m // FK, LN2_B:LN2_B + 1])
            last.then_inc(s["b1_sum"], 1)
            mm(bank[3][0:1, :], last_cols[0:D, 1:2], woutt[0:D, :]).then_inc(s["bout_sum"], 1)
            h_in(0)
            for c in range(2, NC):
                for t in range(c * TPC, (c + 1) * TPC):
                    turn_x(t)
                h_in(c - 1)
            pe.wait_ge(s["bout_made"], 1)
            h_in(NC - 1)

            pe.wait_ge(s["means_made"], 3)
            pe.wait_ge(s["h_made"], NC)
            with pe.Fori(0, L) as l:
                for c in range(NC):
                    pe.wait_ge(s["h_made"], l * NC + c + 1)
                    mm(bank[c][:, :], centre[:, :], h[:, c * C:(c + 1) * C]).then_inc(s["centred"], 1)
                for c in range(NC):
                    pe.wait_ge(s["squared"], l * 2 * NC + c + 1)
                    mm(bank[4 + c][:, :], mean_p[:, :], sq[:, c, :]).then_inc(s["averaged"], 1)
                pe.wait_ge(s["layer_cols"], l + 1)
                for c in range(NC):
                    if c < NC - 1:
                        pe.wait_ge(s["scanned"], l * NC + c + 1)
                        mm(bank[4 + c][:, 0:1], turn[:, :], g[:, c, C - 1:C]).then_inc(s["rotated"], 1)
                    pe.wait_ge(s["damped"], l * NC + c + 1)
                    mm(bank[c][0:D, :], scale_add[:, :], xn[:, c, :]).then_inc(s["mixed"], 1)
                for c in range(NC):
                    pe.wait_ge(s["h_mid"], l * NC + c + 1)
                    mm(bank[4 + c][:, :], centre[:, :], h[:, c * C:(c + 1) * C]).then_inc(s["centred"], 1)
                for c in range(NC):
                    pe.wait_ge(s["squared"], l * 2 * NC + NC + c + 1)
                    mm(bank[c][:, :], mean_d[:, :], sq[0:D, c, :]).then_inc(s["averaged"], 1)
                pe.wait_ge(s["w_copied"], 2 * l + 2)
                for c in range(NC):
                    pe.wait_ge(s["normed2"], l * NC + c + 1)
                    for k in range(FK):
                        last = mm(bank[4 * k + c][:, :], w1t[:, k * P:(k + 1) * P], g[0:D, c, :])
                    last.then_inc(s["spread"], 1)
                for c in range(NC):
                    pe.wait_ge(s["ff_made"], l * NC + c + 1)
                    for k in range(FK):
                        last = mm(bank[c][0:D, :], w2t[:, k, :], ff[:, c, k, :], k == 0, k == FK - 1)
                    last.then_inc(s["ff_back"], 1)
            for c in range(NC):
                pe.wait_ge(s["h_made"], L * NC + c + 1)
                mm(bank[c][:, :], centre[:, :], h[:, c * C:(c + 1) * C]).then_inc(s["centred"], 1)
            for c in range(NC):
                pe.wait_ge(s["squared"], L * 2 * NC + c + 1)
                mm(bank[4 + c][:, :], mean_d[:, :], sq[0:D, c, :]).then_inc(s["averaged"], 1)

            def turn_x1(t):
                pe.wait_ge(s["x1_made"], t + 1)
                if t >= 4:
                    pe.wait_ge(s["x1_lo"], t - 3)
                for k in range(KT):
                    last = pe.transpose(bank[4 + t % 4][:, k * P:(k + 1) * P], x[:, t, k * P:(k + 1) * P], ident[:, :])
                last.then_inc(s["x1_turned"], 1)

            pe.wait_ge(s["last_normed"], NC)
            for t in range(NT + 3):
                if t < NT:
                    if t >= 4:
                        pe.wait_ge(s["x_added"], t - 3)
                    mm(bank[t % 4][:, :], hn[:, t * P:(t + 1) * P], woutt[:, :]).then_inc(s["attn_out"], 1)
                if t >= 3:
                    turn_x1(t - 3)

            def exact3(dst, w, v, start, stop):
                mm(dst, w[0], v[0], start, False)
                mm(dst, w[0], v[1], False, False)
                return mm(dst, w[1], v[0], False, stop)

            def ffn(b, i, k, n):
                jd = n // CS
                pe.wait_ge(s[f"gate_in{b}"], i * (16 * JG) + 16 * JG)
                for q in range(KT):
                    last = pe.transpose(bank[2][:, q * P:q * P + n], stage_gate[b][0:n, q * P:(q + 1) * P], ident[0:n, 0:n])
                last.then_inc(s["turned_stage"], 1)
                pe.wait_ge(s[f"up_in{b}"], i * (16 * JG) + 16 * JG)
                for q in range(KT):
                    last = pe.transpose(bank[3][:, q * P:q * P + n], stage_up[b][0:n, q * P:(q + 1) * P], ident[0:n, 0:n])
                last.then_inc(s["turned_stage"], 1)
                pe.wait_ge(s[f"down_in{b}"], i * (16 * KT * JD) + 16 * KT * jd)
                for q in range(KT):
                    last = pe.transpose(bank[4][0:n, q * P:(q + 1) * P], stage_down[b][:, q, 0:n], ident[:, :])
                last.then_inc(s["turned_stage"], 1)
                pe.wait_ge(s["w_hi"], 3 * k + 3)
                pe.wait_ge(s["w_lo"], 3 * k + 3)
                pe.sem_inc(s["stage_free"], 3)
                for c in range(NC):
                    tok = slice(c * C, (c + 1) * C)
                    for w, dst, read, made in ((wg, 0, "gate_silu", "gate_made"), (wu, 1, "product", "up_made")):
                        if c:
                            pe.wait_ge(s[read], NC * k + c)
                        for q in range(KT):
                            last = exact3(bank[dst][0:n, :], (w[b][0][:, q, 0:n], w[b][1][:, q, 0:n]),
                                          (x1t_hi[:, q, tok], x1t_lo[:, q, tok]), q == 0, q == KT - 1)
                        last.then_inc(s[made], 1)
                for t in range(NT):
                    if t % TPC == 0:
                        pe.wait_ge(s["act_hi_made"], NC * k + t // TPC + 1)
                        pe.wait_ge(s["act_lo_made"], NC * k + t // TPC + 1)
                    if t >= 3:
                        pe.wait_ge(s["down_added"], NT * k + t - 2)
                    tok = slice(t * P, (t + 1) * P)
                    exact3(bank[5 + t % 3][:, :], (act_hi[0:n, tok], act_lo[0:n, tok]), (wd[b][0][0:n, :], wd[b][1][0:n, :]),
                           True, True).then_inc(s["down_made"], 1)

            pe.wait_ge(s["x1_hi"], NT)
            pe.wait_ge(s["x1_lo"], NT)
            with pe.Fori(0, FULL // 2) as i:
                for b in range(2):
                    ffn(b, i, 2 * i + b, P)
            ffn(0, FULL // 2, FULL, REST)

        @block.vector
        def _(v):
            chained = [0]

            def link(ins):
                chained[0] += 1
                ins.then_inc(s["link"], 1)
                v.wait_ge(s["link"], chained[0])

            def tt(o, x0, x1, op):
                return v.tensor_tensor(o, x0, x1, op)

            v.memset(eps[:, :], EPS).then_inc(s["eps_made"], 1)
            v.memset(mean_p[:, :], 1.0 / P).then_inc(s["means_made"], 1)
            v.memset(mean_d[:, :], 1.0 / D).then_inc(s["means_made"], 1)
            v.memset(hn[D:D + 1, :], 1.0)
            v.memset(sgn[0:D, :], 1.0)
            v.memset(sgn[D:P, :], -1.0)
            v.memset(tab[0:D, :, 0:1], 1.0)
            v.memset(tab[D:P, :, 0:1], 0.0)
            v.memset(tabq[0:D, :, 0:1], 0.0)
            link(v.memset(tabq[D:P, :, 0:1], 1.0))
            v.wait_ge(s["masks_made"], 5)
            v.tensor_scalar(centre[:, 0:D], ident[0:D, 0:D], -1.0 / D, None, ALU.add)
            v.tensor_scalar(centre[:, D:P], ident[0:D, 0:D], -1.0 / D, None, ALU.add).then_inc(s["means_made"], 1)
            v.wait_ge(s["turned_w"], 1)
            v.tensor_copy(cols[:, :, 0:PER_LAYER], bank[0][:, 0:NL].rearrange("p (l k) -> p l k", l=L))
            v.tensor_copy(last_cols[:, :], bank[0][:, NL:ROWS]).then_inc(s["cols_made"], 1)
            v.wait_ge(s["cols_made"], 1)
            re, im = cols[:, :, PHZ_RE], cols[:, :, PHZ_IM]
            S = [small[:, n, :] for n in range(12)]
            v.scalar_tensor_tensor(S[0], re, -1.0, re, ALU.mult, ALU.max)
            link(v.scalar_tensor_tensor(S[1], im, -1.0, im, ALU.mult, ALU.max))
            link(tt(S[2], S[0], S[1], ALU.max))
            v.tensor_scalar(S[0], S[2], TINY, None, ALU.max)
            v.tensor_scalar(S[3], S[2], TINY, None, ALU.is_ge)
            link(v.tensor_scalar(S[4], S[2], TINY, None, ALU.is_lt))
            link(v.reciprocal(S[1], S[0]))
            v.tensor_tensor(S[5], re, S[1], ALU.mult)
            link(v.tensor_tensor(S[6], im, S[1], ALU.mult))
            link(tt(S[0], S[5], S[3], ALU.mult))
            v.tensor_tensor(S[6], S[6], S[3], ALU.mult)
            link(tt(S[5], S[0], S[4], ALU.add))
            v.tensor_tensor(S[0], S[5], S[5], ALU.mult)
            link(tt(S[1], S[6], S[6], ALU.mult))
            tt(S[7], S[0], S[1], ALU.add).then_inc(s["q_made"], 1)

            v.wait_ge(s["turned_w"], 2)
            v.tensor_copy(w1t_all[:, 0:2, :].rearrange("d l f -> d (l f)"), bank[1][0:D, :]).then_inc(s["w_kept"], 1)
            v.wait_ge(s["turned_w"], 3)
            v.tensor_copy(w1t_all[:, 2:4, :].rearrange("d l f -> d (l f)"), bank[2][0:D, :]).then_inc(s["w_kept"], 1)
            v.wait_ge(s["turned_w"], 4)
            v.tensor_copy(w2t_all[:, :, :, :].rearrange("p l k d -> p (l k d)"), bank[3][:, :]).then_inc(s["w_kept"], 1)
            v.wait_ge(s["turned_w"], 5)
            v.tensor_copy(wint[:, :, :].rearrange("p k d -> p (k d)"), bank[1][:, 0:KT * D]).then_inc(s["w_kept"], 1)
            v.wait_ge(s["turned_w"], 6)
            v.tensor_copy(woutt[0:D, :], bank[2][0:D, :]).then_inc(s["w_kept"], 1)

            v.wait_ge(s["phase_sqrt"], 1)
            tt(S[9], S[2], S[8], ALU.mult).then_inc(s["mag_made"], 1)
            link(v.reciprocal(S[3], S[8]))

            def unit(k, x0, y0):
                tt(S[0], x0, x0, ALU.mult)
                link(tt(S[1], y0, y0, ALU.mult))
                link(tt(S[4], S[0], S[1], ALU.add))
                link(v.tensor_scalar(S[0], S[4], -0.5, 1.5, ALU.mult, ALU.add))
                tt(cosp[:, :, k], x0, S[0], ALU.mult)
                link(tt(sinp[:, :, k], y0, S[0], ALU.mult))

            tt(S[10], S[5], S[3], ALU.mult)
            link(tt(S[11], S[6], S[3], ALU.mult))
            unit(0, S[10], S[11])
            for k in range(9):
                w = 1 << k
                cw = cosp[:, :, k:k + 1].to_broadcast([P, L, w])
                sw = sinp[:, :, k:k + 1].to_broadcast([P, L, w])
                old, new = slice(0, w), slice(w, 2 * w)
                ta, tb = tmp[:, :, 0:w], tmp[:, :, C // 2:C // 2 + w]
                tt(ta, tab[:, :, old], cw, ALU.mult)
                link(tt(tb, tabq[:, :, old], sw, ALU.mult))
                link(tt(tab[:, :, new], ta, tb, ALU.subtract))
                if k < 8:
                    tt(ta, tab[:, :, old], sw, ALU.mult)
                    link(tt(tb, tabq[:, :, old], cw, ALU.mult))
                    tt(tabq[:, :, new], ta, tb, ALU.add)
                tt(S[0], cosp[:, :, k], cosp[:, :, k], ALU.mult)
                tt(S[1], sinp[:, :, k], sinp[:, :, k], ALU.mult)
                link(v.scalar_tensor_tensor(S[11], cosp[:, :, k], 2.0, sinp[:, :, k], ALU.mult, ALU.mult))
                link(tt(S[10], S[0], S[1], ALU.subtract))
                unit(k + 1, S[10], S[11])
            sg = sgn[:, 0:1].to_broadcast([P, L])
            v.tensor_copy(cols[:, :, COS_C], cosp[:, :, 9])
            tt(cols[:, :, SIN_C], sinp[:, :, 9], sg, ALU.mult)
            tt(S[0], cols[:, :, LC_RE], tab[:, :, 1], ALU.mult)
            link(tt(S[1], cols[:, :, LC_IM], tabq[:, :, 1], ALU.mult))
            link(tt(S[4], S[0], S[1], ALU.subtract))
            tt(cols[:, :, STATE0], S[4], sg, ALU.mult)
            v.wait_ge(s["b1_sum"], 1)
            v.tensor_tensor(cols[:, :, B1P:B1P + FK], cols[:, :, B1:B1 + FK], bank[0][:, 0:L * FK].rearrange("p (l k) -> p l k", l=L),
                            ALU.add).then_inc(s["b1_made"], 1)
            v.wait_ge(s["bout_sum"], 1)
            v.wait_ge(s["bout_in"], 16)
            tt(woutt[D:D + 1, :], bank[3][0:1, :], bout_row[:, :], ALU.add).then_inc(s["bout_made"], 1)
            v.wait_ge(s["b1_made"], 1)
            v.wait_ge(s["phase_tanh"], 1)

            with v.Fori(0, L) as l:
                v.wait_ge(s["h_made"], l * NC + NC)
                v.tensor_copy(tab_l[:, :], tab[:, bass.ds(l, 1), :].rearrange("p o c -> p (o c)"))
                v.tensor_copy(lay[:, :], cols[:, bass.ds(l, 1), :].rearrange("p o c -> p (o c)")).then_inc(s["lay_kept"], 1)
                v.wait_ge(s["lay_kept"], l + 1)
                v.tensor_scalar(turn_a[:, :], perm[:, :], lay[:, SIN_C:SIN_C + 1], None, ALU.mult).then_inc(s["turn_begun"], 1)
                v.tensor_scalar(scale_add[:, :], dup_ident[:, :], lay[:, SC_LIN:SC_LIN + 1], None, ALU.mult)
                v.wait_ge(s["turn_begun"], l + 1)
                v.scalar_tensor_tensor(turn[:, :], ident[:, :], lay[:, COS_C:COS_C + 1], turn_a[:, :], ALU.mult, ALU.add
                                       ).then_inc(s["layer_cols"], 1)
                for c in range(NC):
                    v.wait_ge(s["rooted"], l * 2 * NC + c + 1)
                    tt(xn[:, c, :], bank[c][:, :], rs[:, c, :], ALU.mult).then_inc(s["normed"], 1)
                for c in range(NC):
                    v.wait_ge(s["silu_made"], l * NC + c + 1)
                    tt(xn[:, c, :], sq[:, c, :], tab_l[:, :], ALU.mult).then_inc(s["turned_back"], 1)
                    v.wait_ge(s["turned_back"], l * NC + c + 1)
                    if c:
                        v.wait_ge(s["rotated"], l * (NC - 1) + c)
                    state = bank[4 + c - 1][:, 0:1] if c else lay[:, STATE0:STATE0 + 1]
                    v.tensor_tensor_scan(g[:, c, :], lay[:, DECAY:DECAY + 1].to_broadcast([P, C]), xn[:, c, :], state,
                                         ALU.mult, ALU.add).then_inc(s["scanned"], 1)
                    v.wait_ge(s["scanned"], l * NC + c + 1)
                    tt(xn[:, c, :], g[:, c, :], tab_l[:, :], ALU.mult).then_inc(s["damped"], 1)
                for c in range(NC):
                    v.wait_ge(s["mixed"], l * NC + c + 1)
                    hc = h[:, c * C:(c + 1) * C]
                    tt(hc, hc, bank[c][0:D, :], ALU.add).then_inc(s["h_mid"], 1)
                for c in range(NC):
                    v.wait_ge(s["rooted"], l * 2 * NC + NC + c + 1)
                    v.scalar_tensor_tensor(g[0:D, c, :], bank[4 + c][0:D, :], lay[0:D, LN2_W:LN2_W + 1], rs[0:D, c, :],
                                           ALU.mult, ALU.mult).then_inc(s["normed2"], 1)
                for c in range(NC):
                    v.wait_ge(s["ff_back"], l * NC + c + 1)
                    hc = h[:, c * C:(c + 1) * C]
                    v.scalar_tensor_tensor(hc, bank[c][0:D, :], lay[0:D, B2:B2 + 1], hc, ALU.add, ALU.add).then_inc(s["h_made"], 1)
            for c in range(NC):
                v.wait_ge(s["rooted"], L * 2 * NC + c + 1)
                v.scalar_tensor_tensor(hn[0:D, c * C:(c + 1) * C], bank[c][0:D, :], last_cols[0:D, 0:1], rs[0:D, c, :],
                                       ALU.mult, ALU.mult).then_inc(s["last_normed"], 1)

            def measure(t, n):
                v.bn_stats(stats[:, t, :], x[:, t, :]).then_inc(s["stats_made"], 1)
                v.wait_ge(s["stats_made"], n + 1)
                v.bn_aggr(mv[:, t, :], stats[:, t, :]).then_inc(s["aggregated"], 1)

            def normalize(t, n, signal):
                v.wait_ge(s["rstd_made"], n + 1)
                v.tensor_scalar(x[:, t, :], x[:, t, :], mv[:, t, 0:1], rstd[:, t:t + 1], ALU.subtract, ALU.mult).then_inc(s[signal], 1)

            def keep_lo(t):
                v.wait_ge(s["x1_hi"], t + 1)
                tt(x1t_lo[:, :, t * P:(t + 1) * P], bank[4 + t % 4][:, :].rearrange("p (k n) -> p k n", k=KT),
                   x1t_hi[:, :, t * P:(t + 1) * P].bitcast(F32), ALU.subtract).then_inc(s["x1_lo"], 1)

            for t in range(NT + 4):
                if t < NT:
                    v.wait_ge(s["attn_out"], t + 1)
                    tt(x[:, t, :], x[:, t, :], bank[t % 4][:, :], ALU.add).then_inc(s["x_added"], 1)
                    v.wait_ge(s["x_added"], t + 1)
                    measure(t, t)
                if 1 <= t <= NT:
                    normalize(t - 1, t - 1, "x1_made")
                if t >= 4:
                    keep_lo(t - 4)

            def ffn(b, k, n, final):
                for m, w in enumerate((wg, wu)):
                    v.wait_ge(s["w_hi"], 3 * k + m + 1)
                    tt(w[b][1][:, :, 0:n], bank[2 + m][:, :].rearrange("p (k n) -> p k n", k=KT)[:, :, 0:n],
                       w[b][0][:, :, 0:n].bitcast(F32), ALU.subtract).then_inc(s["w_lo"], 1)
                v.wait_ge(s["w_hi"], 3 * k + 3)
                tt(wd[b][1][0:n, :], bank[4][0:n, :], wd[b][0][0:n, :].bitcast(F32), ALU.subtract).then_inc(s["w_lo"], 1)
                for c in range(NC + 1):
                    if c < NC:
                        v.wait_ge(s["gate_silu"], NC * k + c + 1)
                        v.wait_ge(s["up_made"], NC * k + c + 1)
                        if c >= 2:
                            v.wait_ge(s["act_hi_made"], NC * k + c - 1)
                            v.wait_ge(s["act_lo_made"], NC * k + c - 1)
                        tt(prod[0:n, c % 2, :], silu[0:n, c % 2, :], bank[1][0:n, :], ALU.mult).then_inc(s["product"], 1)
                    if c:
                        v.wait_ge(s["act_hi_made"], NC * k + c)
                        tok = slice((c - 1) * C, c * C)
                        tt(act_lo[0:n, tok], prod[0:n, (c - 1) % 2, :], act_hi[0:n, tok].bitcast(F32), ALU.subtract
                           ).then_inc(s["act_lo_made"], 1)
                for t in range(NT + final):
                    if t < NT:
                        v.wait_ge(s["down_made"], NT * k + t + 1)
                        tt(x[:, t, :], x[:, t, :], bank[5 + t % 3][:, :], ALU.add).then_inc(s["down_added"], 1)
                        if final:
                            v.wait_ge(s["down_added"], NT * k + t + 1)
                            measure(t, NT + t)
                    if final and t:
                        normalize(t - 1, NT + t - 1, "out_normed")

            with v.Fori(0, FULL // 2) as i:
                for b in range(2):
                    ffn(b, 2 * i + b, P, False)
            ffn(0, FULL, REST, True)


_INS = ["L0_attn_x", "L0_attn_Win", "L0_attn_bin", "L0_attn_ln1_w", "L0_attn_ln1_b", "L0_attn_phz_re", "L0_attn_phz_im",
        "L0_attn_lc_re", "L0_attn_lc_im", "L0_attn_sc_lin", "L0_attn_ln2_w", "L0_attn_ln2_b", "L0_attn_W1", "L0_attn_b1",
        "L0_attn_W2", "L0_attn_b2", "L0_attn_lnl_w", "L0_attn_lnl_b", "L0_attn_Wout", "L0_attn_bout", "L0_ffn_codebook",
        "L0_ffn_idx_gate", "L0_ffn_idx_up", "L0_ffn_idx_down"]


def kernel(**inputs):
    import concourse.bacc as bacc
    from concourse.bass_utils import run_bass_kernel_spmd

    nc = bacc.Bacc("TRN2", target_bir_lowering=False, num_devices=1)
    arrays, args = {}, {}
    for name in _INS:
        array = np.ascontiguousarray(inputs[name])
        arrays[f"in_{name}"] = array
        args[name] = nc.dram_tensor(f"in_{name}", array.shape, mybir.dt.from_np(array.dtype), kind="ExternalInput").ap()
    shape = inputs["L0_attn_x"].shape
    out = nc.dram_tensor("out_x", shape, F32, kind="ExternalOutput").ap()
    build(nc, args, out)
    result = run_bass_kernel_spmd(nc, [arrays], core_ids=[0])
    return result.results[0]["out_x"]
```

```python
from contextlib import ExitStack

import numpy as np
import concourse.bass as bass
from concourse import mybir

F32 = mybir.dt.float32
F32R = mybir.dt.float32r
I32 = mybir.dt.int32
U16 = mybir.dt.uint16
ALU = mybir.AluOpType
ACT = mybir.ActivationFunctionType

P = 128
EPS = 1e-5
TINY = 1e-30

LN1_W, LN1_B, SC_LIN, LN2_W, LN2_B, B2, PHZ_RE, PHZ_IM, LC_RE, LC_IM, B1 = range(11)
PER_LAYER = 12
COS_C, SIN_C, DECAY, STATE0, B1P = 12, 13, 14, 15, 16
LAYER_COLS = 18



def build(nc, a, out):
    L, D = a["L0_attn_ln1_w"].shape
    T, V = a["L0_attn_x"].shape[1:]
    FF = a["L0_attn_W1"].shape[1]
    CB, CS = a["L0_ffn_codebook"].shape
    INNER = a["L0_ffn_idx_gate"].shape[0]
    C = 512
    NC = T // C
    NT = T // P
    TPC = C // P
    KT = V // P
    FK = FF // P
    FULL = INNER // P
    REST = INNER - FULL * P
    JG = V // CS
    JD = P // CS
    JH = JG // 2
    JP = JG + JH
    GROUPS = JP // JD
    QUADS = JP // 4
    TILES = FULL + 1
    LOW = 512
    LT = LOW // P
    HIGH = CB // LOW
    AHEAD = 2
    NL = L * PER_LAYER
    LNL_W, LNL_B, BIN, ROWS = NL, NL + 1, NL + 2, NL + 3

    x_in = a["L0_attn_x"][0].rearrange("(t p) v -> p t v", p=P)
    y_out = out[0].rearrange("(t p) v -> p t v", p=P)

    ctx = ExitStack()
    attn_ctx = ExitStack()
    parts = nc.dram_tensor("index_parts", (TILES, 2, JP, P), U16).ap()
    with ctx:
        def sb(name, shape, dt=F32, where=ctx):
            return where.enter_context(nc.sbuf_tensor(name, shape, dt))

        def sem(name):
            return ctx.enter_context(nc.semaphore(name))

        bank = [ctx.enter_context(nc.psum_tensor(f"bank{i}", [P, 512], F32)) for i in range(8)]

        x = sb("x", [P, NT, V])
        x1t_hi = sb("x1t_hi", [P, KT, T], F32R)
        ident = sb("ident", [P, P])
        stage_gate = [sb(f"stage_gate{b}", [P, V // 2]) for b in range(2)]
        stage_down = [sb(f"stage_down{b}", [P, KT, P]) for b in range(2)]
        idx_gate = [sb(f"idx_gate{b}", [P, JH], I32) for b in range(2)]
        idx_down = [sb(f"idx_down{b}", [P, KT, JD], I32) for b in range(2)]
        stats = sb("stats", [P, NT, 6])
        mv = sb("mv", [P, NT, 2])
        rstd = sb("rstd", [P, NT])
        eps = sb("eps", [P, 1])
        book = [sb(f"book{p}", [P, LT, CS * HIGH], F32R) for p in range(2)]
        adder = sb("adder", [P, 2 * P - CS], F32R)
        low_of = sb("low_of", [P, LT])
        high_of = sb("high_of", [P, 1])

        with attn_ctx:
            def at(name, shape, dt=F32):
                return sb(name, shape, dt, attn_ctx)

            sq = at("sq", [P, NC, C])
            rs = at("rs", [P, NC, C])
            xn = at("xn", [P, NC, C])
            g = at("g", [P, NC, C])
            h = at("h", [D, T])
            ff = at("ff", [P, NC, FK, C])
            hn = at("hn", [D + 1, T])
            woutt = at("woutt", [D + 1, V])
            book_in = at("book_in", [P, HIGH, LT, CS])
            adder_in = at("adder_in", [P, 2 * P - CS])
            iota_low = at("iota_low", [P, LT], I32)
            iota_m = at("iota_m", [P, 1], I32)
            parts_t = at("parts_t", [JP, TILES, 2, P], U16)
            rows = at("rows", [ROWS, P])
            cols = at("cols", [P, L, LAYER_COLS])
            last_cols = at("last_cols", [P, 3])
            lay = at("lay", [P, LAYER_COLS])
            tab = at("tab", [P, L, C])
            tab_l = at("tab_l", [P, C])
            cosp = at("cosp", [P, L, 10])
            sinp = at("sinp", [P, L, 10])
            small = at("small", [P, 12, L])
            sgn = at("sgn", [P, 1])
            perm = at("perm", [P, P])
            dup_ident = at("dup_ident", [P, D])
            centre = at("centre", [D, P])
            mean_p = at("mean_p", [P, P])
            mean_d = at("mean_d", [D, P])
            turn = at("turn", [P, P])
            turn_a = at("turn_a", [P, P])
            scale_add = at("scale_add", [P, D])
            w1_in = at("w1_in", [P, L * FK, D])
            w2_in = at("w2_in", [D, L, FF])
            win_in = at("win_in", [D, V])
            wout_in = at("wout_in", [P, KT, D])
            w1t_all = at("w1t_all", [D, L, FF])
            w2t_all = at("w2t_all", [P, L, FK, D])
            w1t = at("w1t", [D, FF])
            w2t = at("w2t", [P, FK, D])
            wint = at("wint", [P, KT, D])
            bout_row = at("bout_row", [1, V])

        xt, tabq, tmp = ff, g, xn
        high_f, low_f = (b[:, :, :].rearrange("p c n -> p (c n)")[:, 0:TILES * JP] for b in (sq, rs))
        high_i, low_i = (b[:, :, :].bitcast(I32).rearrange("p c n -> p (c n)")[:, 0:TILES * JP] for b in (sq, rs))
        picked_idx = high_i.rearrange("p (k j) -> p k j", k=TILES)

        x1t_lo = sb("x1t_lo", [P, KT, T], F32R)
        wg = [sb(f"wg{b}", [P, 2, KT, P], F32R) for b in range(2)]
        wu = [sb(f"wu{b}", [P, 2, KT, P], F32R) for b in range(2)]
        wd = [sb(f"wd{b}", [P, 2, V], F32R) for b in range(2)]
        prod = sb("prod", [P, 2, C])
        act_hi = sb("act_hi", [P, 2, T], F32R)
        act_lo = sb("act_lo", [P, 2, T], F32R)
        one_hot = [sb(f"one_hot{b}", [P, LT, 4 * P], F32R) for b in range(2)]
        chosen = [sb(f"chosen{b}", [P, 2, 4 * P], F32R) for b in range(2)]
        bc = [sb(f"bc{b}", [P, 2, 8 * P], U16) for b in range(2)]

        sem_names = """idx_rows_in0 idx_rows_in1 gate_in0 gate_in1 down_in0 down_in1
            x_in0 x_in1 x_in2 x_in3 rows_in w_in bout_in consts_made masks_made turned_w turned_x x_kept h_made bout_made
            cols_made phase_sqrt phase_tanh q_made mag_made link b1_sum b1_made tables_made layer_cols w_copied
            centred squared averaged rooted normed silu_made rotated scanned damped mixed h_mid normed2
            spread ff_made ff_back last_normed attn_out x_added aggregated rstd_made x1_made x1_turned x1_hi x1_lo
            stage_free turned_stage w_hi w_lo gate_made up_made gate_silu product act_hi_made act_lo_made
            down_made down_added out_normed stored h_sum book_in idx_in idx_cleared idx_split parts_turned
            parts_kept parts_out bc_in0 bc_in1 one_hot_made candidates chosen_made summed picked_kept iotas_made book_made w_kept eps_made means_made bout_sum
            stage_claimed spread_claimed rows_claimed lay_kept turn_begun turned_back stats_made""".split()
        s = {n: sem(n) for n in sem_names}

        ROW_DMAS = 2 * 10 + FK + 2 * 3
        block = ctx.enter_context(nc.Block())

        @block.sync
        def _(sp):
            ig, iu = a["L0_ffn_idx_gate"], a["L0_ffn_idx_up"]
            idn = a["L0_ffn_idx_down"].rearrange("(q p) j -> p q j", p=P)
            last = FULL * P

            def index_rows(b, k, waited):
                if waited is not None:
                    sp.wait_ge(s[f"gate_in{b}"], waited * (16 * JH))
                    sp.sem_inc(s["rows_claimed"], 1)
                    sp.wait_ge(s[f"down_in{b}"], waited * (16 * KT * JD))
                    sp.sem_inc(s["rows_claimed"], 1)
                sp.dma_start(idx_gate[b][:, :], ig[bass.ds(k * P, P), JH:JG]).then_inc(s[f"idx_rows_in{b}"], 16)
                sp.dma_start(idx_down[b][:, :, :], idn[:, :, bass.ds(k * JD, JD)]).then_inc(s[f"idx_rows_in{b}"], 16)

            def last_index_rows(b, waited):
                sp.wait_ge(s[f"gate_in{b}"], waited * (16 * JH))
                sp.wait_ge(s[f"down_in{b}"], waited * (16 * KT * JD))
                sp.dma_start(idx_gate[b][0:REST, :], ig[last:INNER, JH:JG]).then_inc(s[f"idx_rows_in{b}"], 16)
                sp.dma_start(idx_down[b][:, :, 0:REST // CS], idn[:, :, FULL * JD:]).then_inc(s[f"idx_rows_in{b}"], 16)

            def spread_parts(k):
                for e in range(QUADS // 2):
                    if e >= 2 or not (isinstance(k, int) and k == 0):
                        sp.wait_ge(s["chosen_made"], k * QUADS + 2 * e - 2)
                        sp.sem_inc(s["spread_claimed"], 1)
                    src = parts[bass.ds(k, 1), :, 8 * e:8 * e + 8, :].rearrange("o m j p -> o m (j p)").to_broadcast([P, 2, 8 * P])
                    sp.dma_start(bc[e % 2][:, :, :], src).then_inc(s[f"bc_in{e % 2}"], 16)

            sp.dma_start(picked_idx[:, 0:FULL, 0:JG], iu[0:last, :].rearrange("(k p) j -> p k j", p=P)).then_inc(s["idx_in"], 16)
            sp.dma_start(picked_idx[:, 0:FULL, JG:JP], ig[0:last, 0:JH].rearrange("(k p) j -> p k j", p=P)).then_inc(s["idx_in"], 16)
            index_rows(0, 0, None)
            index_rows(1, 1, None)
            sp.wait_ge(s["idx_cleared"], 1)
            sp.dma_start(picked_idx[0:REST, FULL, 0:JG], iu[last:INNER, :]).then_inc(s["idx_in"], 16)
            sp.dma_start(picked_idx[0:REST, FULL, JG:JP], ig[last:INNER, 0:JH]).then_inc(s["idx_in"], 16)
            per_layer = ["L0_attn_ln1_w", "L0_attn_ln1_b", "L0_attn_sc_lin", "L0_attn_ln2_w", "L0_attn_ln2_b", "L0_attn_b2",
                         "L0_attn_phz_re", "L0_attn_phz_im", "L0_attn_lc_re", "L0_attn_lc_im"]
            for n, name in enumerate(per_layer):
                for half in range(2):
                    sp.dma_start(rows[n:NL:PER_LAYER, half * D:(half + 1) * D], a[name]).then_inc(s["rows_in"], 16)
            for k in range(FK):
                sp.dma_start(rows[B1 + k:NL:PER_LAYER, :], a["L0_attn_b1"][:, k * P:(k + 1) * P]).then_inc(s["rows_in"], 16)
            for n, name in ((LNL_W, "L0_attn_lnl_w"), (LNL_B, "L0_attn_lnl_b"), (BIN, "L0_attn_bin")):
                for half in range(2):
                    sp.dma_start(rows[n:n + 1, half * D:(half + 1) * D], a[name].rearrange("(o d) -> o d", o=1)).then_inc(s["rows_in"], 16)
            for half in range(2):
                sp.dma_start(book_in[:, 8 * half:8 * half + 8, :, :],
                             a["L0_ffn_codebook"][half * CB // 2:(half + 1) * CB // 2, :].rearrange("(h k p) e -> p h k e", k=LT, p=P)
                             ).then_inc(s["book_in"], 16)
            for k in range(TILES):
                sp.wait_ge(s["parts_kept"], k + 1)
                sp.dma_start(parts[k].rearrange("m j p -> j m p"), parts_t[:, k, :, :]).then_inc(s["parts_out"], 16)
            sp.wait_ge(s["parts_out"], 16 * TILES)
            sp.wait_ge(s["x1_lo"], NT)
            spread_parts(0)
            with sp.Fori(0, FULL // 2 - 1) as i:
                for b in range(2):
                    index_rows(b, 2 * i + 2 + b, i + 1)
                    spread_parts(2 * i + 1 + b)
            last_index_rows(0, FULL // 2)
            for k in (FULL - 1, FULL):
                spread_parts(k)
            for t in range(NT):
                sp.wait_ge(s["out_normed"], t + 1)
                sp.dma_start(y_out[:, t, :], x[:, t, :]).then_inc(s["stored"], 16)
            sp.wait_ge(s["stored"], 16 * NT)

        @block.gpsimd
        def _(pool):
            pool.memset(ident[:, :], 0.0).then_inc(s["consts_made"], 1)
            pool.memset(perm[:, :], 0.0).then_inc(s["consts_made"], 1)
            pool.memset(dup_ident[:, :], 0.0).then_inc(s["consts_made"], 1)
            pool.wait_ge(s["consts_made"], 3)
            pool.affine_select(out=ident[:, :], in_=ident[:, :], compare_op=ALU.not_equal, fill=1.0, base=0,
                               pattern=[[-1, P]], channel_multiplier=1).then_inc(s["masks_made"], 1)
            for base, m in ((-D, perm), (D, perm), (0, dup_ident), (-D, dup_ident)):
                if base == D or (base == -D and m is dup_ident):
                    pool.wait_ge(s["masks_made"], 2 if m is perm else 4)
                pool.affine_select(out=m[:, :], in_=m[:, :], compare_op=ALU.not_equal, fill=1.0, base=base,
                                   pattern=[[-1, m.shape[1]]], channel_multiplier=1).then_inc(s["masks_made"], 1)
            pool.memset(adder_in[:, :], 0.0).then_inc(s["consts_made"], 1)
            pool.wait_ge(s["consts_made"], 4)
            block8 = adder_in[:, P - CS:P]
            pool.memset(block8, 1.0).then_inc(s["consts_made"], 1)
            pool.iota(iota_low[:, :], pattern=[[P, LT]], base=0, channel_multiplier=1).then_inc(s["iotas_made"], 1)
            pool.iota(iota_m[:, :], pattern=[[0, 1]], base=0, channel_multiplier=1).then_inc(s["iotas_made"], 1)
            pool.wait_ge(s["consts_made"], 5)
            pool.affine_select(out=block8, in_=block8, compare_op=ALU.is_ge, fill=0.0, base=0,
                               pattern=[[-HIGH, CS]], channel_multiplier=1).then_inc(s["masks_made"], 1)
            pool.wait_ge(s["masks_made"], 6)
            pool.affine_select(out=block8, in_=block8, compare_op=ALU.is_ge, fill=0.0, base=HIGH - 1,
                               pattern=[[HIGH, CS]], channel_multiplier=-1).then_inc(s["masks_made"], 1)
            pool.sem_inc(s["stage_free"], 4)

            def gather(dst, idx, sm):
                pool.indirect_dma_start(dst, None, a["L0_ffn_codebook"],
                                        bass.IndirectOffsetOnAxis(ap=idx, axis=0)).then_inc(sm, 16)

            def gathers(b, arrived, freed, n, jd):
                pool.wait_ge(s[f"idx_rows_in{b}"], arrived)
                pool.wait_ge(s["stage_free"], freed)
                pool.sem_inc(s["stage_claimed"], 1)
                for q in range(KT):
                    for j in range(jd):
                        gather(stage_down[b][:, q, j * CS:(j + 1) * CS], idx_down[b][:, q, j:j + 1], s[f"down_in{b}"])
                for j in range(JH):
                    gather(stage_gate[b][0:n, j * CS:(j + 1) * CS], idx_gate[b][0:n, j:j + 1], s[f"gate_in{b}"])

            with pool.Fori(0, FULL // 2) as i:
                for b in range(2):
                    gathers(b, i * 32 + 32, i * 4 + 2 * b + 2, P, JD)
            gathers(0, (FULL // 2) * 32 + 32, 2 * FULL + 2, REST, REST // CS)

        @block.scalar
        def _(act):
            for c in range(NC):
                act.dma_start(x[:, c * TPC:(c + 1) * TPC, :], x_in[:, c * TPC:(c + 1) * TPC, :]).then_inc(s[f"x_in{c}"], 16)
            act.dma_start(win_in[:, :], a["L0_attn_Win"]).then_inc(s["w_in"], 16)
            act.dma_start(w1_in[:, :, :], a["L0_attn_W1"].rearrange("l (k p) d -> p (l k) d", p=P)).then_inc(s["w_in"], 16)
            act.dma_start(w2_in[:, :, :], a["L0_attn_W2"].rearrange("l d f -> d l f")).then_inc(s["w_in"], 16)
            act.dma_start(wout_in[:, :, :], a["L0_attn_Wout"].rearrange("(k p) d -> p k d", p=P)).then_inc(s["w_in"], 16)
            act.dma_start(bout_row[:, :], a["L0_attn_bout"].rearrange("(o v) -> o v", o=1)).then_inc(s["bout_in"], 16)

            def keep_x(t):
                act.wait_ge(s["turned_x"], t + 1)
                c = t // TPC
                if c >= 2:
                    act.wait_ge(s["h_sum"], c - 1)
                act.activation(xt[:, c % 2 * 2:c % 2 * 2 + 2, :, (t % TPC) * P:(t % TPC + 1) * P],
                               bank[4 + t % 4][:, :].rearrange("p (a b n) -> p a b n", a=2, b=2), ACT.Copy).then_inc(s["x_kept"], 1)

            def keep_h(c):
                act.wait_ge(s["h_sum"], c + 1)
                act.activation(h[:, c * C:(c + 1) * C], bank[c][0:D, :], ACT.Identity, bias=last_cols[0:D, 2:3]).then_inc(s["h_made"], 1)

            for t in range(TPC):
                keep_x(t)
            act.wait_ge(s["q_made"], 1)
            act.activation(small[:, 8, :], small[:, 7, :], ACT.Sqrt).then_inc(s["phase_sqrt"], 1)
            for t in range(TPC, 2 * TPC):
                keep_x(t)
            act.wait_ge(s["mag_made"], 1)
            act.activation(cols[:, :, DECAY], small[:, 9, :], ACT.Tanh).then_inc(s["phase_tanh"], 1)
            act.wait_ge(s["cols_made"], 1)
            keep_h(0)
            for c in range(2, NC):
                for t in range(c * TPC, (c + 1) * TPC):
                    keep_x(t)
                keep_h(c - 1)
            keep_h(NC - 1)

            for k in range(TILES):
                act.wait_ge(s["parts_turned"], k + 1)
                act.activation(parts_t[:, k, :, :], bank[4 + k % 4][0:JP, 0:2 * P].rearrange("j (m p) -> j m p", m=2),
                               ACT.Copy).then_inc(s["parts_kept"], 1)

            def root(dst, src):
                return act.activation(dst, src, ACT.Abs_reciprocal_sqrt, bias=eps[0:dst.shape[0], :])

            act.wait_ge(s["eps_made"], 1)
            with act.Fori(0, L) as l:
                act.wait_ge(s["h_made"], l * NC + NC)
                act.wait_ge(s["w_kept"], 5)
                act.activation(w1t[:, :], w1t_all[:, bass.ds(l, 1), :].rearrange("d o f -> d (o f)"), ACT.Copy).then_inc(s["w_copied"], 1)
                act.activation(w2t[:, :, :].rearrange("p k d -> p (k d)"),
                               w2t_all[:, bass.ds(l, 1), :, :].rearrange("p o k d -> p (o k d)"), ACT.Copy).then_inc(s["w_copied"], 1)
                for c in range(NC):
                    act.wait_ge(s["centred"], l * 2 * NC + c + 1)
                    act.activation(sq[:, c, :], bank[c][:, :], ACT.Square).then_inc(s["squared"], 1)
                for c in range(NC):
                    act.wait_ge(s["averaged"], l * 2 * NC + c + 1)
                    root(rs[:, c, :], bank[4 + c][:, :]).then_inc(s["rooted"], 1)
                act.wait_ge(s["layer_cols"], l + 1)
                for c in range(NC):
                    act.wait_ge(s["normed"], l * NC + c + 1)
                    act.activation(sq[:, c, :], xn[:, c, :], ACT.Silu, bias=lay[:, LN1_B:LN1_B + 1],
                                   scale=lay[:, LN1_W:LN1_W + 1]).then_inc(s["silu_made"], 1)
                for c in range(NC):
                    act.wait_ge(s["centred"], l * 2 * NC + NC + c + 1)
                    act.activation(sq[0:D, c, :], bank[4 + c][0:D, :], ACT.Square).then_inc(s["squared"], 1)
                for c in range(NC):
                    act.wait_ge(s["averaged"], l * 2 * NC + NC + c + 1)
                    root(rs[0:D, c, :], bank[c][0:D, :]).then_inc(s["rooted"], 1)
                for c in range(NC):
                    act.wait_ge(s["spread"], l * NC + c + 1)
                    for k in range(FK):
                        last = act.activation(ff[:, c, k, :], bank[4 * k + c][:, :], ACT.Silu, bias=lay[:, B1P + k:B1P + k + 1])
                    last.then_inc(s["ff_made"], 1)
            for c in range(NC):
                act.wait_ge(s["centred"], L * 2 * NC + c + 1)
                act.activation(sq[0:D, c, :], bank[c][0:D, :], ACT.Square).then_inc(s["squared"], 1)
            for c in range(NC):
                act.wait_ge(s["averaged"], L * 2 * NC + c + 1)
                root(rs[0:D, c, :], bank[4 + c][0:D, :]).then_inc(s["rooted"], 1)

            def keep_x1(t):
                act.wait_ge(s["x1_turned"], t + 1)
                act.activation(x1t_hi[:, :, t * P:(t + 1) * P], bank[4 + t % 4][:, :].rearrange("p (k n) -> p k n", k=KT),
                               ACT.Copy).then_inc(s["x1_hi"], 1)

            for t in range(NT + 2):
                if t < NT:
                    act.wait_ge(s["aggregated"], t + 1)
                    root(rstd[:, t:t + 1], mv[:, t, 1:2]).then_inc(s["rstd_made"], 1)
                if t >= 2:
                    keep_x1(t - 2)

            def keep_picked(b, k, g):
                act.wait_ge(s["summed"], k * QUADS + 4 * g + 4)
                w, q = (wu[b], g) if g < KT else (wg[b], g - KT)
                act.activation(w[:, :, q, :], bank[3][:, 0:2 * P].rearrange("p (m n) -> p m n", m=2), ACT.Copy).then_inc(s["picked_kept"], 1)

            def turned_hi(b, k, n):
                act.wait_ge(s["turned_stage"], 2 * k + 1)
                act.activation(wd[b][0:n, 0, :], bank[2][0:n, :], ACT.Copy).then_inc(s["w_hi"], 1)
                act.wait_ge(s["turned_stage"], 2 * k + 2)
                act.activation(wg[b][:, 0, 2:KT, 0:n], bank[0][:, 0:2 * P].rearrange("p (k n) -> p k n", k=2)[:, :, 0:n],
                               ACT.Copy).then_inc(s["w_hi"], 1)

            def silu(b, k, n, c):
                act.wait_ge(s["gate_made"], NC * k + c + 1)
                act.wait_ge(s["act_lo_made"], NC * k + c - 1 + AHEAD)
                act.activation(prod[0:n, c % 2, :], bank[0][0:n, :], ACT.Silu).then_inc(s["gate_silu"], 1)

            def product_hi(b, k, n, c):
                act.wait_ge(s["product"], NC * k + c + 1)
                act.activation(act_hi[0:n, b, c * C:(c + 1) * C], prod[0:n, c % 2, :], ACT.Copy).then_inc(s["act_hi_made"], 1)

            for g in range(GROUPS):
                keep_picked(0, 0, g)
            with act.Fori(0, FULL // 2) as i:
                for b in range(2):
                    k = 2 * i + b
                    turned_hi(b, k, P)
                    for slot in range(QUADS):
                        step, c = (3, slot // 6) if b == 0 else (1, slot // 2)
                        if c < NC and slot % (2 * step) == step:
                            silu(b, k, P, c)
                        if c < NC and slot % (2 * step) == 2 * step - 1:
                            product_hi(b, k, P, c)
                        if slot % 4 == 0 and slot:
                            keep_picked(1 - b, k + 1, slot // 4 - 1)
                    keep_picked(1 - b, k + 1, GROUPS - 1)
            turned_hi(0, FULL, REST)
            for c in range(NC):
                silu(0, FULL, REST, c)
                product_hi(0, FULL, REST, c)
            for t in range(NT):
                act.wait_ge(s["aggregated"], NT + t + 1)
                root(rstd[:, t:t + 1], mv[:, t, 1:2]).then_inc(s["rstd_made"], 1)

        @block.tensor
        def _(pe):
            def mm(dst, lhs, rhs, start=True, stop=True):
                return pe.matmul(dst, lhs, rhs, start=start, stop=stop)

            pe.wait_ge(s["masks_made"], 1)
            pe.wait_ge(s["rows_in"], 16 * ROW_DMAS)
            pe.transpose(bank[0][:, 0:ROWS], rows[:, :], ident[0:ROWS, 0:ROWS]).then_inc(s["turned_w"], 1)

            def turn_x(t):
                if t % TPC == 0:
                    pe.wait_ge(s[f"x_in{t // TPC}"], 16)
                if t >= 4:
                    pe.wait_ge(s["x_kept"], t - 3)
                for k in range(KT):
                    last = pe.transpose(bank[4 + t % 4][:, k * P:(k + 1) * P], x[:, t, k * P:(k + 1) * P], ident[:, :])
                last.then_inc(s["turned_x"], 1)

            def h_in(c):
                pe.wait_ge(s["x_kept"], (c + 1) * TPC)
                if c == 0:
                    pe.wait_ge(s["w_kept"], 5)
                    pe.wait_ge(s["b1_made"], 1)
                for k in range(KT):
                    last = mm(bank[c][0:D, :], wint[:, k, :], xt[:, c % 2 * 2 + k // 2, k % 2, :], k == 0, k == KT - 1)
                last.then_inc(s["h_sum"], 1)

            for t in range(TPC):
                turn_x(t)
            pe.wait_ge(s["w_in"], 64)
            for half in range(2):
                for n in range(4):
                    m = half * 4 + n
                    last = pe.transpose(bank[1 + half][0:D, n * P:(n + 1) * P], w1_in[:, m, :], ident[:, :])
                last.then_inc(s["turned_w"], 1)
            for m in range(L * FK):
                last = pe.transpose(bank[3][:, m * D:(m + 1) * D], w2_in[:, m // FK, (m % FK) * P:(m % FK + 1) * P], ident[0:D, 0:D])
            last.then_inc(s["turned_w"], 1)
            pe.wait_ge(s["w_kept"], 2)
            for k in range(KT):
                last = pe.transpose(bank[1][:, k * D:(k + 1) * D], win_in[:, k * P:(k + 1) * P], ident[0:D, 0:D])
            last.then_inc(s["turned_w"], 1)
            for k in range(KT):
                last = pe.transpose(bank[2][0:D, k * P:(k + 1) * P], wout_in[:, k, :], ident[:, :])
            last.then_inc(s["turned_w"], 1)
            for t in range(TPC, 2 * TPC):
                turn_x(t)
            pe.wait_ge(s["cols_made"], 1)
            pe.wait_ge(s["w_kept"], 5)
            for m in range(L * FK):
                last = mm(bank[0][:, m:m + 1], w1t_all[:, m // FK, (m % FK) * P:(m % FK + 1) * P], cols[0:D, m // FK, LN2_B:LN2_B + 1])
            last.then_inc(s["b1_sum"], 1)
            mm(bank[3][0:1, :], last_cols[0:D, 1:2], woutt[0:D, :]).then_inc(s["bout_sum"], 1)
            h_in(0)
            for c in range(2, NC):
                for t in range(c * TPC, (c + 1) * TPC):
                    turn_x(t)
                h_in(c - 1)
            pe.wait_ge(s["bout_made"], 1)
            h_in(NC - 1)
            pe.wait_ge(s["idx_split"], 1)
            for k in range(TILES):
                if k < 4:
                    pe.wait_ge(s["x_kept"], NT)
                else:
                    pe.wait_ge(s["parts_kept"], k - 3)
                for m, part in enumerate((low_f, high_f)):
                    last = pe.transpose(bank[4 + k % 4][0:JP, m * P:(m + 1) * P], part[:, k * JP:(k + 1) * JP], ident[:, :])
                last.then_inc(s["parts_turned"], 1)
            pe.wait_ge(s["parts_kept"], TILES)

            pe.wait_ge(s["means_made"], 3)
            pe.wait_ge(s["h_made"], NC)
            with pe.Fori(0, L) as l:
                for c in range(NC):
                    pe.wait_ge(s["h_made"], l * NC + c + 1)
                    mm(bank[c][:, :], centre[:, :], h[:, c * C:(c + 1) * C]).then_inc(s["centred"], 1)
                for c in range(NC):
                    pe.wait_ge(s["squared"], l * 2 * NC + c + 1)
                    mm(bank[4 + c][:, :], mean_p[:, :], sq[:, c, :]).then_inc(s["averaged"], 1)
                pe.wait_ge(s["layer_cols"], l + 1)
                for c in range(NC):
                    if c < NC - 1:
                        pe.wait_ge(s["scanned"], l * NC + c + 1)
                        mm(bank[4 + c][:, 0:1], turn[:, :], g[:, c, C - 1:C]).then_inc(s["rotated"], 1)
                    pe.wait_ge(s["damped"], l * NC + c + 1)
                    mm(bank[c][0:D, :], scale_add[:, :], xn[:, c, :]).then_inc(s["mixed"], 1)
                for c in range(NC):
                    pe.wait_ge(s["h_mid"], l * NC + c + 1)
                    mm(bank[4 + c][:, :], centre[:, :], h[:, c * C:(c + 1) * C]).then_inc(s["centred"], 1)
                for c in range(NC):
                    pe.wait_ge(s["squared"], l * 2 * NC + NC + c + 1)
                    mm(bank[c][:, :], mean_d[:, :], sq[0:D, c, :]).then_inc(s["averaged"], 1)
                pe.wait_ge(s["w_copied"], 2 * l + 2)
                for c in range(NC):
                    pe.wait_ge(s["normed2"], l * NC + c + 1)
                    for k in range(FK):
                        last = mm(bank[4 * k + c][:, :], w1t[:, k * P:(k + 1) * P], g[0:D, c, :])
                    last.then_inc(s["spread"], 1)
                for c in range(NC):
                    pe.wait_ge(s["ff_made"], l * NC + c + 1)
                    for k in range(FK):
                        last = mm(bank[c][0:D, :], w2t[:, k, :], ff[:, c, k, :], k == 0, k == FK - 1)
                    last.then_inc(s["ff_back"], 1)
            for c in range(NC):
                pe.wait_ge(s["h_made"], L * NC + c + 1)
                mm(bank[c][:, :], centre[:, :], h[:, c * C:(c + 1) * C]).then_inc(s["centred"], 1)
            for c in range(NC):
                pe.wait_ge(s["squared"], L * 2 * NC + c + 1)
                mm(bank[4 + c][:, :], mean_d[:, :], sq[0:D, c, :]).then_inc(s["averaged"], 1)

            def turn_x1(t):
                pe.wait_ge(s["x1_made"], t + 1)
                if t >= 4:
                    pe.wait_ge(s["x1_lo"], t - 3)
                for k in range(KT):
                    last = pe.transpose(bank[4 + t % 4][:, k * P:(k + 1) * P], x[:, t, k * P:(k + 1) * P], ident[:, :])
                last.then_inc(s["x1_turned"], 1)

            pe.wait_ge(s["last_normed"], NC)
            for t in range(NT + 3):
                if t < NT:
                    if t >= 4:
                        pe.wait_ge(s["x_added"], t - 3)
                    mm(bank[t % 4][:, :], hn[:, t * P:(t + 1) * P], woutt[:, :]).then_inc(s["attn_out"], 1)
                if t >= 3:
                    turn_x1(t - 3)

            def exact3(dst, w, v, start, stop):
                mm(dst, w[0], v[0], start, False)
                mm(dst, w[0], v[1], False, False)
                return mm(dst, w[1], v[0], False, stop)

            def candidates(k, slot):
                pe.wait_ge(s["one_hot_made"], k * QUADS + slot + 1)
                if slot >= 2 or not isinstance(k, int):
                    pe.wait_ge(s["chosen_made"], k * QUADS + slot - 1)
                for m in range(2):
                    for q in range(LT):
                        last = mm(bank[4 + 2 * (slot % 2) + m][:, :], book[m][:, q, :], one_hot[slot % 2][:, q, :], q == 0, q == LT - 1)
                last.then_inc(s["candidates"], 1)

            def add_up(k, slot):
                pe.wait_ge(s["chosen_made"], k * QUADS + slot + 1)
                if slot % 4 == 0 and (slot or not isinstance(k, int)):
                    pe.wait_ge(s["picked_kept"], k * GROUPS + slot // 4)
                for jj in range(4):
                    j = slot % 4 * 4 + jj
                    last = mm(bank[3][:, 0:2 * P].rearrange("p (m n) -> p m n", m=2), adder[:, P - CS - CS * j:2 * P - CS - CS * j],
                              chosen[slot % 2][:, :, jj * P:(jj + 1) * P], j == 0, j == JD - 1)
                last.then_inc(s["summed"], 1)

            def turn_stage(b, i, k, n):
                if b == 0:
                    pe.wait_ge(s["down_added"], NT * i + AHEAD)
                pe.wait_ge(s[f"down_in{b}"], i * (16 * KT * JD) + 16 * KT * (n // CS))
                for q in range(KT):
                    last = pe.transpose(bank[2][0:n, q * P:(q + 1) * P], stage_down[b][:, q, 0:n], ident[:, :])
                last.then_inc(s["turned_stage"], 1)
                if b:
                    pe.wait_ge(s["gate_silu"], NC * k)
                pe.wait_ge(s[f"gate_in{b}"], i * (16 * JH) + 16 * JH)
                for q in range(2):
                    last = pe.transpose(bank[0][:, q * P:q * P + n], stage_gate[b][0:n, q * P:(q + 1) * P], ident[0:n, 0:n])
                last.then_inc(s["turned_stage"], 1)

            def hidden(b, k, n, c, w, dst, made, read):
                if c:
                    pe.wait_ge(s[read], NC * k + c)
                tok = slice(c * C, (c + 1) * C)
                for q in range(KT):
                    last = exact3(bank[dst][0:n, :], (w[b][:, 0, q, 0:n], w[b][:, 1, q, 0:n]),
                                  (x1t_hi[:, q, tok], x1t_lo[:, q, tok]), q == 0, q == KT - 1)
                last.then_inc(s[made], 1)

            def up(b, k, n, c):
                if c == 0:
                    pe.wait_ge(s["picked_kept"], k * GROUPS + GROUPS)
                hidden(b, k, n, c, wu, 1, "up_made", "product")

            def gate(b, k, n, c):
                if c == 0:
                    pe.wait_ge(s["w_hi"], 2 * k + 2)
                    pe.wait_ge(s["w_lo"], 2 * k + 2)
                    pe.sem_inc(s["stage_free"], 2)
                hidden(b, k, n, c, wg, 0, "gate_made", "gate_silu")

            def down(i, k, n, tiles, t, banks):
                if t % TPC == 0:
                    pe.wait_ge(s["act_hi_made"], NC * k + t // TPC + 1)
                    pe.wait_ge(s["act_lo_made"], NC * k + t // TPC + 1 + AHEAD)
                if t >= len(banks):
                    pe.wait_ge(s["down_added"], NT * i + t + 1 - len(banks) + AHEAD)
                tok = slice(t * P, (t + 1) * P)
                for b in range(tiles):
                    last = exact3(bank[banks[t % len(banks)]][:, :], (act_hi[0:n, b, tok], act_lo[0:n, b, tok]),
                                  (wd[b][0:n, 0, :], wd[b][0:n, 1, :]), b == 0, b == tiles - 1)
                last.then_inc(s["down_made"], 1)

            pe.wait_ge(s["x1_hi"], NT)
            pe.wait_ge(s["x1_lo"], NT)
            for slot in range(QUADS):
                candidates(0, slot)
                if slot:
                    add_up(0, slot - 1)
            add_up(0, QUADS - 1)
            with pe.Fori(0, FULL // 2) as i:
                for b in range(2):
                    k = 2 * i + b
                    turn_stage(b, i, k, P)
                    for slot in range(QUADS):
                        candidates(k + 1, slot)
                        if slot:
                            add_up(k + 1, slot - 1)
                        step = 3 if b == 0 else 1
                        if slot % step == 0 and slot // step < 2 * NC:
                            (gate if slot // step % 2 else up)(b, k, P, slot // step // 2)
                        if b and slot >= 2 * NC:
                            down(i, k, P, 2, slot - 2 * NC, (2,))
                    add_up(k + 1, QUADS - 1)
            turn_stage(0, FULL // 2, FULL, REST)
            for c in range(NC):
                up(0, FULL, REST, c)
                gate(0, FULL, REST, c)
            for t in range(NT):
                down(FULL // 2, FULL, REST, 1, t, (2, 4, 5, 6))

        @block.vector
        def _(v):
            chained = [0]

            def link(ins):
                chained[0] += 1
                ins.then_inc(s["link"], 1)
                v.wait_ge(s["link"], chained[0])

            def tt(o, x0, x1, op):
                return v.tensor_tensor(o, x0, x1, op)

            v.sem_inc(s["act_lo_made"], AHEAD)
            v.sem_inc(s["down_added"], AHEAD)
            v.memset(picked_idx[REST:P, FULL, :], 0).then_inc(s["idx_cleared"], 1)
            v.memset(eps[:, :], EPS).then_inc(s["eps_made"], 1)
            v.memset(mean_p[:, :], 1.0 / P).then_inc(s["means_made"], 1)
            v.memset(mean_d[:, :], 1.0 / D).then_inc(s["means_made"], 1)
            v.memset(hn[D:D + 1, :], 1.0)
            v.memset(sgn[0:D, :], 1.0)
            v.memset(sgn[D:P, :], -1.0)
            v.memset(tab[0:D, :, 0:1], 1.0)
            v.memset(tab[D:P, :, 0:1], 0.0)
            v.memset(tabq[0:D, :, 0:1], 0.0)
            link(v.memset(tabq[D:P, :, 0:1], 1.0))
            v.wait_ge(s["masks_made"], 5)
            v.tensor_scalar(centre[:, 0:D], ident[0:D, 0:D], -1.0 / D, None, ALU.add)
            v.tensor_scalar(centre[:, D:P], ident[0:D, 0:D], -1.0 / D, None, ALU.add).then_inc(s["means_made"], 1)
            v.wait_ge(s["turned_w"], 1)
            v.tensor_copy(cols[:, :, 0:PER_LAYER], bank[0][:, 0:NL].rearrange("p (l k) -> p l k", l=L))
            v.tensor_copy(last_cols[:, :], bank[0][:, NL:ROWS]).then_inc(s["cols_made"], 1)
            v.wait_ge(s["cols_made"], 1)
            re, im = cols[:, :, PHZ_RE], cols[:, :, PHZ_IM]
            S = [small[:, n, :] for n in range(12)]
            v.scalar_tensor_tensor(S[0], re, -1.0, re, ALU.mult, ALU.max)
            link(v.scalar_tensor_tensor(S[1], im, -1.0, im, ALU.mult, ALU.max))
            link(tt(S[2], S[0], S[1], ALU.max))
            v.tensor_scalar(S[0], S[2], TINY, None, ALU.max)
            v.tensor_scalar(S[3], S[2], TINY, None, ALU.is_ge)
            link(v.tensor_scalar(S[4], S[2], TINY, None, ALU.is_lt))
            link(v.reciprocal(S[1], S[0]))
            v.tensor_tensor(S[5], re, S[1], ALU.mult)
            link(v.tensor_tensor(S[6], im, S[1], ALU.mult))
            link(tt(S[0], S[5], S[3], ALU.mult))
            v.tensor_tensor(S[6], S[6], S[3], ALU.mult)
            link(tt(S[5], S[0], S[4], ALU.add))
            v.tensor_tensor(S[0], S[5], S[5], ALU.mult)
            link(tt(S[1], S[6], S[6], ALU.mult))
            tt(S[7], S[0], S[1], ALU.add).then_inc(s["q_made"], 1)

            v.wait_ge(s["idx_in"], 64)
            link(v.tensor_scalar(low_i, high_i, LOW - 1, None, ALU.bitwise_and))
            v.tensor_copy(low_f, low_i)
            link(v.tensor_scalar(high_i, high_i, LOW.bit_length() - 1, None, ALU.logical_shift_right))
            v.tensor_copy(high_f, high_i).then_inc(s["idx_split"], 1)

            v.wait_ge(s["turned_w"], 2)
            v.tensor_copy(w1t_all[:, 0:2, :].rearrange("d l f -> d (l f)"), bank[1][0:D, :]).then_inc(s["w_kept"], 1)
            v.wait_ge(s["turned_w"], 3)
            v.tensor_copy(w1t_all[:, 2:4, :].rearrange("d l f -> d (l f)"), bank[2][0:D, :]).then_inc(s["w_kept"], 1)
            v.wait_ge(s["turned_w"], 4)
            v.tensor_copy(w2t_all[:, :, :, :].rearrange("p l k d -> p (l k d)"), bank[3][:, :]).then_inc(s["w_kept"], 1)
            v.wait_ge(s["turned_w"], 5)
            v.tensor_copy(wint[:, :, :].rearrange("p k d -> p (k d)"), bank[1][:, 0:KT * D]).then_inc(s["w_kept"], 1)
            v.wait_ge(s["turned_w"], 6)
            v.tensor_copy(woutt[0:D, :], bank[2][0:D, :]).then_inc(s["w_kept"], 1)

            v.wait_ge(s["phase_sqrt"], 1)
            tt(S[9], S[2], S[8], ALU.mult).then_inc(s["mag_made"], 1)
            link(v.reciprocal(S[3], S[8]))

            def unit(k, x0, y0):
                tt(S[0], x0, x0, ALU.mult)
                link(tt(S[1], y0, y0, ALU.mult))
                link(tt(S[4], S[0], S[1], ALU.add))
                link(v.tensor_scalar(S[0], S[4], -0.5, 1.5, ALU.mult, ALU.add))
                tt(cosp[:, :, k], x0, S[0], ALU.mult)
                link(tt(sinp[:, :, k], y0, S[0], ALU.mult))

            tt(S[10], S[5], S[3], ALU.mult)
            link(tt(S[11], S[6], S[3], ALU.mult))
            unit(0, S[10], S[11])
            for k in range(9):
                w = 1 << k
                cw = cosp[:, :, k:k + 1].to_broadcast([P, L, w])
                sw = sinp[:, :, k:k + 1].to_broadcast([P, L, w])
                old, new = slice(0, w), slice(w, 2 * w)
                ta, tb = tmp[:, :, 0:w], tmp[:, :, C // 2:C // 2 + w]
                tt(ta, tab[:, :, old], cw, ALU.mult)
                link(tt(tb, tabq[:, :, old], sw, ALU.mult))
                link(tt(tab[:, :, new], ta, tb, ALU.subtract))
                if k < 8:
                    tt(ta, tab[:, :, old], sw, ALU.mult)
                    link(tt(tb, tabq[:, :, old], cw, ALU.mult))
                    tt(tabq[:, :, new], ta, tb, ALU.add)
                tt(S[0], cosp[:, :, k], cosp[:, :, k], ALU.mult)
                tt(S[1], sinp[:, :, k], sinp[:, :, k], ALU.mult)
                link(v.scalar_tensor_tensor(S[11], cosp[:, :, k], 2.0, sinp[:, :, k], ALU.mult, ALU.mult))
                link(tt(S[10], S[0], S[1], ALU.subtract))
                unit(k + 1, S[10], S[11])
            sg = sgn[:, 0:1].to_broadcast([P, L])
            v.tensor_copy(cols[:, :, COS_C], cosp[:, :, 9])
            tt(cols[:, :, SIN_C], sinp[:, :, 9], sg, ALU.mult)
            tt(S[0], cols[:, :, LC_RE], tab[:, :, 1], ALU.mult)
            link(tt(S[1], cols[:, :, LC_IM], tabq[:, :, 1], ALU.mult))
            link(tt(S[4], S[0], S[1], ALU.subtract))
            tt(cols[:, :, STATE0], S[4], sg, ALU.mult)
            v.wait_ge(s["b1_sum"], 1)
            v.tensor_tensor(cols[:, :, B1P:B1P + FK], cols[:, :, B1:B1 + FK], bank[0][:, 0:L * FK].rearrange("p (l k) -> p l k", l=L),
                            ALU.add).then_inc(s["b1_made"], 1)
            v.wait_ge(s["iotas_made"], 2)
            v.wait_ge(s["masks_made"], 7)
            v.wait_ge(s["book_in"], 32)
            v.tensor_copy(low_of[:, :], iota_low[:, :])
            link(v.tensor_scalar(iota_m[:, :], iota_m[:, :], HIGH - 1, None, ALU.bitwise_and))
            v.tensor_copy(high_of[:, :], iota_m[:, :])
            v.tensor_copy(adder[:, :], adder_in[:, :])
            for q in range(LT):
                link(v.tensor_copy(book[0][:, q, :].rearrange("p (e h) -> p h e", e=CS), book_in[:, :, q, :]))
                tt(book[1][:, q, :].rearrange("p (e h) -> p h e", e=CS), book_in[:, :, q, :],
                   book[0][:, q, :].rearrange("p (e h) -> p h e", e=CS).bitcast(F32), ALU.subtract).then_inc(s["book_made"], 1)
            v.wait_ge(s["bout_sum"], 1)
            v.wait_ge(s["bout_in"], 16)
            tt(woutt[D:D + 1, :], bank[3][0:1, :], bout_row[:, :], ALU.add).then_inc(s["bout_made"], 1)
            v.wait_ge(s["b1_made"], 1)
            v.wait_ge(s["phase_tanh"], 1)

            with v.Fori(0, L) as l:
                v.wait_ge(s["h_made"], l * NC + NC)
                v.tensor_copy(tab_l[:, :], tab[:, bass.ds(l, 1), :].rearrange("p o c -> p (o c)"))
                v.tensor_copy(lay[:, :], cols[:, bass.ds(l, 1), :].rearrange("p o c -> p (o c)")).then_inc(s["lay_kept"], 1)
                v.wait_ge(s["lay_kept"], l + 1)
                v.tensor_scalar(turn_a[:, :], perm[:, :], lay[:, SIN_C:SIN_C + 1], None, ALU.mult).then_inc(s["turn_begun"], 1)
                v.tensor_scalar(scale_add[:, :], dup_ident[:, :], lay[:, SC_LIN:SC_LIN + 1], None, ALU.mult)
                v.wait_ge(s["turn_begun"], l + 1)
                v.scalar_tensor_tensor(turn[:, :], ident[:, :], lay[:, COS_C:COS_C + 1], turn_a[:, :], ALU.mult, ALU.add
                                       ).then_inc(s["layer_cols"], 1)
                for c in range(NC):
                    v.wait_ge(s["rooted"], l * 2 * NC + c + 1)
                    tt(xn[:, c, :], bank[c][:, :], rs[:, c, :], ALU.mult).then_inc(s["normed"], 1)
                for c in range(NC):
                    v.wait_ge(s["silu_made"], l * NC + c + 1)
                    tt(xn[:, c, :], sq[:, c, :], tab_l[:, :], ALU.mult).then_inc(s["turned_back"], 1)
                    v.wait_ge(s["turned_back"], l * NC + c + 1)
                    if c:
                        v.wait_ge(s["rotated"], l * (NC - 1) + c)
                    state = bank[4 + c - 1][:, 0:1] if c else lay[:, STATE0:STATE0 + 1]
                    v.tensor_tensor_scan(g[:, c, :], lay[:, DECAY:DECAY + 1].to_broadcast([P, C]), xn[:, c, :], state,
                                         ALU.mult, ALU.add).then_inc(s["scanned"], 1)
                    v.wait_ge(s["scanned"], l * NC + c + 1)
                    tt(xn[:, c, :], g[:, c, :], tab_l[:, :], ALU.mult).then_inc(s["damped"], 1)
                for c in range(NC):
                    v.wait_ge(s["mixed"], l * NC + c + 1)
                    hc = h[:, c * C:(c + 1) * C]
                    tt(hc, hc, bank[c][0:D, :], ALU.add).then_inc(s["h_mid"], 1)
                for c in range(NC):
                    v.wait_ge(s["rooted"], l * 2 * NC + NC + c + 1)
                    v.scalar_tensor_tensor(g[0:D, c, :], bank[4 + c][0:D, :], lay[0:D, LN2_W:LN2_W + 1], rs[0:D, c, :],
                                           ALU.mult, ALU.mult).then_inc(s["normed2"], 1)
                for c in range(NC):
                    v.wait_ge(s["ff_back"], l * NC + c + 1)
                    hc = h[:, c * C:(c + 1) * C]
                    v.scalar_tensor_tensor(hc, bank[c][0:D, :], lay[0:D, B2:B2 + 1], hc, ALU.add, ALU.add).then_inc(s["h_made"], 1)
            for c in range(NC):
                v.wait_ge(s["rooted"], L * 2 * NC + c + 1)
                v.scalar_tensor_tensor(hn[0:D, c * C:(c + 1) * C], bank[c][0:D, :], last_cols[0:D, 0:1], rs[0:D, c, :],
                                       ALU.mult, ALU.mult).then_inc(s["last_normed"], 1)

            def measure(t, n):
                v.bn_stats(stats[:, t, :], x[:, t, :]).then_inc(s["stats_made"], 1)
                v.wait_ge(s["stats_made"], n + 1)
                v.bn_aggr(mv[:, t, :], stats[:, t, :]).then_inc(s["aggregated"], 1)

            def normalize(t, n, signal):
                v.wait_ge(s["rstd_made"], n + 1)
                v.tensor_scalar(x[:, t, :], x[:, t, :], mv[:, t, 0:1], rstd[:, t:t + 1], ALU.subtract, ALU.mult).then_inc(s[signal], 1)

            def keep_lo(t):
                v.wait_ge(s["x1_hi"], t + 1)
                tt(x1t_lo[:, :, t * P:(t + 1) * P], bank[4 + t % 4][:, :].rearrange("p (k n) -> p k n", k=KT),
                   x1t_hi[:, :, t * P:(t + 1) * P].bitcast(F32), ALU.subtract).then_inc(s["x1_lo"], 1)

            for t in range(NT + 4):
                if t < NT:
                    v.wait_ge(s["attn_out"], t + 1)
                    tt(x[:, t, :], x[:, t, :], bank[t % 4][:, :], ALU.add).then_inc(s["x_added"], 1)
                    v.wait_ge(s["x_added"], t + 1)
                    measure(t, t)
                if 1 <= t <= NT:
                    normalize(t - 1, t - 1, "x1_made")
                if t >= 4:
                    keep_lo(t - 4)

            def one_hots(k, slot):
                half, at0 = slot // 2, slot % 2 * 4 * P
                if slot % 2 == 0:
                    v.wait_ge(s[f"bc_in{half % 2}"], k * (16 * QUADS // 4) + 16 * (half // 2) + 16)
                if slot >= 2 or not isinstance(k, int):
                    v.wait_ge(s["candidates"], k * QUADS + slot - 1)
                for q in range(LT):
                    last = v.tensor_scalar(one_hot[slot % 2][:, q, :], bc[half % 2][:, 0, at0:at0 + 4 * P], low_of[:, q:q + 1], None,
                                           ALU.is_equal)
                last.then_inc(s["one_hot_made"], 1)

            def choose(k, slot):
                half, at0 = slot // 2, slot % 2 * 4 * P
                v.wait_ge(s["candidates"], k * QUADS + slot + 1)
                if slot >= 2 or not isinstance(k, int):
                    v.wait_ge(s["summed"], k * QUADS + slot - 1)
                for m in range(2):
                    last = v.scalar_tensor_tensor(chosen[slot % 2][:, m, :], bc[half % 2][:, 1, at0:at0 + 4 * P], high_of[:, 0:1],
                                                  bank[4 + 2 * (slot % 2) + m][:, :], ALU.is_equal, ALU.mult)
                last.then_inc(s["chosen_made"], 1)

            def turned_lo(b, k, n):
                v.wait_ge(s["w_hi"], 2 * k + 1)
                tt(wd[b][0:n, 1, :], bank[2][0:n, :], wd[b][0:n, 0, :].bitcast(F32), ALU.subtract).then_inc(s["w_lo"], 1)
                v.wait_ge(s["w_hi"], 2 * k + 2)
                tt(wg[b][:, 1, 2:KT, 0:n], bank[0][:, 0:2 * P].rearrange("p (k n) -> p k n", k=2)[:, :, 0:n],
                   wg[b][:, 0, 2:KT, 0:n].bitcast(F32), ALU.subtract).then_inc(s["w_lo"], 1)

            def product(b, k, n, c):
                v.wait_ge(s["up_made"], NC * k + c + 1)
                v.wait_ge(s["gate_silu"], NC * k + c + 1)
                pc = prod[0:n, c % 2, :]
                tt(pc, pc, bank[1][0:n, :], ALU.mult).then_inc(s["product"], 1)

            def product_lo(b, k, n, c):
                v.wait_ge(s["act_hi_made"], NC * k + c + 1)
                tok = slice(c * C, (c + 1) * C)
                tt(act_lo[0:n, b, tok], prod[0:n, c % 2, :], act_hi[0:n, b, tok].bitcast(F32), ALU.subtract).then_inc(s["act_lo_made"], 1)

            def add_down(i, t, banks):
                v.wait_ge(s["down_made"], NT * i + t + 1)
                tt(x[:, t, :], x[:, t, :], bank[banks[t % len(banks)]][:, :], ALU.add).then_inc(s["down_added"], 1)

            def quad(k, slot):
                if slot == 0:
                    one_hots(k, 0)
                if slot < QUADS - 1:
                    one_hots(k, slot + 1)
                choose(k, slot)

            for slot in range(QUADS):
                quad(0, slot)
            with v.Fori(0, FULL // 2) as i:
                for b in range(2):
                    k = 2 * i + b
                    turned_lo(b, k, P)
                    for slot in range(QUADS):
                        quad(k + 1, slot)
                        step, c = (3, slot // 6) if b == 0 else (1, slot // 2)
                        if c < NC and slot % (2 * step) == step:
                            product(b, k, P, c)
                        if c < NC and slot % (2 * step) == 2 * step - 1:
                            product_lo(b, k, P, c)
                        if b and slot >= 2 * NC:
                            add_down(i, slot - 2 * NC, (2,))
            turned_lo(0, FULL, REST)
            for c in range(NC):
                product(0, FULL, REST, c)
                product_lo(0, FULL, REST, c)
            for t in range(NT + 1):
                if t < NT:
                    add_down(FULL // 2, t, (2, 4, 5, 6))
                    v.wait_ge(s["down_added"], NT * (FULL // 2) + t + 1 + AHEAD)
                    measure(t, NT + t)
                if t:
                    normalize(t - 1, NT + t - 1, "out_normed")


_INS = ["L0_attn_x", "L0_attn_Win", "L0_attn_bin", "L0_attn_ln1_w", "L0_attn_ln1_b", "L0_attn_phz_re", "L0_attn_phz_im",
        "L0_attn_lc_re", "L0_attn_lc_im", "L0_attn_sc_lin", "L0_attn_ln2_w", "L0_attn_ln2_b", "L0_attn_W1", "L0_attn_b1",
        "L0_attn_W2", "L0_attn_b2", "L0_attn_lnl_w", "L0_attn_lnl_b", "L0_attn_Wout", "L0_attn_bout", "L0_ffn_codebook",
        "L0_ffn_idx_gate", "L0_ffn_idx_up", "L0_ffn_idx_down"]


def kernel(**inputs):
    import concourse.bacc as bacc
    from concourse.bass_utils import run_bass_kernel_spmd

    nc = bacc.Bacc("TRN2", target_bir_lowering=False, num_devices=1)
    arrays, args = {}, {}
    for name in _INS:
        array = np.ascontiguousarray(inputs[name])
        arrays[f"in_{name}"] = array
        args[name] = nc.dram_tensor(f"in_{name}", array.shape, mybir.dt.from_np(array.dtype), kind="ExternalInput").ap()
    shape = inputs["L0_attn_x"].shape
    out = nc.dram_tensor("out_x", shape, F32, kind="ExternalOutput").ap()
    build(nc, args, out)
    result = run_bass_kernel_spmd(nc, [arrays], core_ids=[0])
    return result.results[0]["out_x"]
```

```python
from contextlib import ExitStack

import numpy as np
import concourse.bass as bass
from concourse import mybir

F32 = mybir.dt.float32
F32R = mybir.dt.float32r
I32 = mybir.dt.int32
U16 = mybir.dt.uint16
ALU = mybir.AluOpType
ACT = mybir.ActivationFunctionType

P = 128
EPS = 1e-5
TINY = 1e-30

LN1_W, LN1_B, SC_LIN, LN2_W, LN2_B, B2, PHZ_RE, PHZ_IM, LC_RE, LC_IM, B1 = range(11)
PER_LAYER = 12
COS_C, SIN_C, DECAY, STATE0, B1P = 12, 13, 14, 15, 16
LAYER_COLS = 18



def build(nc, a, out):
    L, D = a["L0_attn_ln1_w"].shape
    T, V = a["L0_attn_x"].shape[1:]
    FF = a["L0_attn_W1"].shape[1]
    CB, CS = a["L0_ffn_codebook"].shape
    INNER = a["L0_ffn_idx_gate"].shape[0]
    C = 512
    NC = T // C
    NT = T // P
    TPC = C // P
    KT = V // P
    FK = FF // P
    FULL = INNER // P
    REST = INNER - FULL * P
    JG = V // CS
    JD = P // CS
    JH = JG // 2
    JP = JG + JH
    GROUPS = JP // JD
    QUADS = JP // 4
    TILES = FULL + 1
    PICKED = TILES - 1
    LOW = 512
    LT = LOW // P
    HIGH = CB // LOW
    SHARES = (6, 4)
    TURN_DOWN = (8, 6)
    FIRST_DOWN = 8
    EXTRA = 16
    JE = JP - EXTRA
    AHEAD = 4
    NL = L * PER_LAYER
    LNL_W, LNL_B, BIN, ROWS = NL, NL + 1, NL + 2, NL + 3

    x_in = a["L0_attn_x"][0].rearrange("(t p) v -> p t v", p=P)
    y_out = out[0].rearrange("(t p) v -> p t v", p=P)

    ctx = ExitStack()
    attn_ctx = ExitStack()
    parts = nc.dram_tensor("index_parts", (PICKED + 1, 2, JP, P), U16).ap()
    with ctx:
        def sb(name, shape, dt=F32, where=ctx):
            return where.enter_context(nc.sbuf_tensor(name, shape, dt))

        def sem(name):
            return ctx.enter_context(nc.semaphore(name))

        bank = [ctx.enter_context(nc.psum_tensor(f"bank{i}", [P, 512], F32)) for i in range(8)]

        x = sb("x", [P, NT, V])
        x1t_hi = sb("x1t_hi", [P, KT, T], F32R)
        ident = sb("ident", [P, P])
        stage_gate = [sb(f"stage_gate{b}", [P, V // 2]) for b in range(2)]
        stage_down = [sb(f"stage_down{b}", [P, KT, P]) for b in range(2)]
        idx_gate = [sb(f"idx_gate{b}", [P, JH], I32) for b in range(2)]
        idx_down = [sb(f"idx_down{b}", [P, KT, JD], I32) for b in range(2)]
        stage_more = sb("stage_more", [P, JE * CS])
        idx_more = sb("idx_more", [P, JE], I32)
        stats = sb("stats", [P, NT, 6])
        mv = sb("mv", [P, NT, 2])
        rstd = sb("rstd", [P, NT])
        shift = sb("shift", [P, NT])
        warm = sb("warm", [P, 1])
        eps = sb("eps", [P, 1])
        book = [sb(f"book{p}", [P, LT, CS * HIGH], F32R) for p in range(2)]
        adder = sb("adder", [P, 2 * P - CS], F32R)
        low_of = sb("low_of", [P, LT])
        high_of = sb("high_of", [P, 1])

        with attn_ctx:
            def at(name, shape, dt=F32):
                return sb(name, shape, dt, attn_ctx)

            sq = at("sq", [P, NC, C])
            rs = at("rs", [P, NC, C])
            xn = at("xn", [P, NC, C])
            g = at("g", [P, NC, C])
            h = at("h", [D, T])
            ff = at("ff", [P, NC, FK, C])
            hn = at("hn", [D + 1, T])
            woutt = at("woutt", [D + 1, V])
            book_in = at("book_in", [P, HIGH, LT, CS])
            adder_in = at("adder_in", [P, 2 * P - CS])
            iota_low = at("iota_low", [P, LT], I32)
            iota_m = at("iota_m", [P, 1], I32)
            parts_t = at("parts_t", [JP, PICKED + 1, 2, P], U16)
            rows = at("rows", [ROWS, P])
            cols = at("cols", [P, L, LAYER_COLS])
            last_cols = at("last_cols", [P, 3])
            lay = at("lay", [P, LAYER_COLS])
            tab = at("tab", [P, L, C])
            tab_l = at("tab_l", [P, C])
            cosp = at("cosp", [P, L, 10])
            sinp = at("sinp", [P, L, 10])
            small = at("small", [P, 12, L])
            sgn = at("sgn", [P, 1])
            perm = at("perm", [P, P])
            dup_ident = at("dup_ident", [P, D])
            centre = at("centre", [D, P])
            mean_p = at("mean_p", [P, P])
            mean_d = at("mean_d", [D, P])
            turn = at("turn", [P, P])
            turn_a = at("turn_a", [P, P])
            scale_add = at("scale_add", [P, D])
            w1_in = at("w1_in", [P, L * FK, D])
            w2_in = at("w2_in", [D, L, FF])
            win_in = at("win_in", [D, V])
            wout_in = at("wout_in", [P, KT, D])
            w1t_all = at("w1t_all", [D, L, FF])
            w2t_all = at("w2t_all", [P, L, FK, D])
            w1t = at("w1t", [D, FF])
            w2t = at("w2t", [P, FK, D])
            wint = at("wint", [P, KT, D])
            bout_row = at("bout_row", [1, V])

        xt, tabq, tmp = ff, g, xn
        high_f, low_f = (b[:, :, :].rearrange("p c n -> p (c n)")[:, 0:(PICKED + 1) * JP] for b in (sq, rs))
        high_i, low_i = (b[:, :, :].bitcast(I32).rearrange("p c n -> p (c n)")[:, 0:(PICKED + 1) * JP] for b in (sq, rs))
        picked_idx = high_i.rearrange("p (k j) -> p k j", k=PICKED + 1)

        x1t_lo = sb("x1t_lo", [P, KT, T], F32R)
        wg = [sb(f"wg{b}", [P, 2, KT, P], F32R) for b in range(2)]
        wu = [sb(f"wu{b}", [P, 2, KT, P], F32R) for b in range(2)]
        wd = [sb(f"wd{b}", [P, 2, V], F32R) for b in range(2)]
        prod = sb("prod", [P, 2, C])
        act_hi = sb("act_hi", [P, 2, T], F32R)
        act_lo = sb("act_lo", [P, 2, T], F32R)
        one_hot = [sb(f"one_hot{b}", [P, LT, 4 * P], F32R) for b in range(2)]
        chosen = [sb(f"chosen{b}", [P, 2, 4 * P], F32R) for b in range(2)]
        bc = [sb(f"bc{b}", [P, 2, 4 * P], U16) for b in range(4)]

        sem_names = """gate_index_in0 gate_index_in1 down_index_in0 down_index_in1 gate_in0 gate_in1 down_in0 down_in1
            x_in0 x_in1 x_in2 x_in3 rows_in w_in bout_in consts_made masks_made turned_w turned_x x_kept h_made bout_made
            cols_made phase_sqrt phase_tanh q_made mag_made link b1_sum b1_made layer_cols w_copied
            centred squared averaged rooted normed silu_made rotated scanned damped mixed h_mid normed2
            spread ff_made ff_back last_normed attn_out x_added aggregated rstd_made shift_made warmed x1_made x1_turned x1_hi x1_lo
            turned_stage w_hi w_lo gate_made up_made gate_silu product act_hi_made act_lo_made
            down_made down_added out_normed stored h_sum book_in idx_in idx_cleared idx_split parts_turned
            parts_kept parts_out bc_in0 bc_in1 bc_in2 bc_in3 one_hot_made candidates chosen_made more_in idx_more_in more_turned more_hi more_lo summed picked_kept iotas_made book_made w_kept eps_made means_made bout_sum
            stage_claimed spread_claimed rows_claimed lay_kept turn_begun turned_back stats_made""".split()
        s = {n: sem(n) for n in sem_names}

        ROW_DMAS = 10 + FK + 3

        def quads_before(n, slot):
            return slot if n is None else n * QUADS + slot + EXTRA // 4

        block = ctx.enter_context(nc.Block())

        @block.sync
        def _(sp):
            ig, iu = a["L0_ffn_idx_gate"], a["L0_ffn_idx_up"]
            idn = a["L0_ffn_idx_down"].rearrange("(q p) j -> p q j", p=P)
            last = FULL * P

            def gate_index(b, k, waited):
                if waited is not None:
                    sp.wait_ge(s[f"gate_in{b}"], waited * (16 * JH))
                    sp.sem_inc(s["rows_claimed"], 1)
                sp.dma_start(idx_gate[b][:, :], ig[bass.ds(k * P, P), JH:JG]).then_inc(s[f"gate_index_in{b}"], 16)

            def down_index(b, k, waited):
                if waited is not None:
                    sp.wait_ge(s[f"down_in{b}"], waited * (16 * KT * JD))
                    sp.sem_inc(s["rows_claimed"], 1)
                sp.dma_start(idx_down[b][:, :, :], idn[:, :, bass.ds(k * JD, JD)]).then_inc(s[f"down_index_in{b}"], 16)

            def spread_parts(n, slots):
                for slot in slots:
                    sp.wait_ge(s["chosen_made"], quads_before(n, slot) - 3)
                    sp.sem_inc(s["spread_claimed"], 1)
                    src = parts[bass.ds(n, 1), :, 4 * slot:4 * slot + 4, :].rearrange("o m j p -> o m (j p)").to_broadcast([P, 2, 4 * P])
                    sp.dma_start(bc[slot % 4][:, :, :], src).then_inc(s[f"bc_in{slot % 4}"], 16)

            sp.dma_start(idx_more[:, 0:JG], iu[0:P, :]).then_inc(s["idx_more_in"], 16)
            sp.dma_start(idx_more[:, JG:JE], ig[0:P, 0:JH - EXTRA]).then_inc(s["idx_more_in"], 16)
            per_layer = ["L0_attn_ln1_w", "L0_attn_ln1_b", "L0_attn_sc_lin", "L0_attn_ln2_w", "L0_attn_ln2_b", "L0_attn_b2",
                         "L0_attn_phz_re", "L0_attn_phz_im", "L0_attn_lc_re", "L0_attn_lc_im"]
            for n, name in enumerate(per_layer):
                sp.dma_start(rows[n:NL:PER_LAYER, :].rearrange("l (o d) -> l o d", o=2),
                             a[name].rearrange("l (o d) -> l o d", o=1).to_broadcast([L, 2, D])).then_inc(s["rows_in"], 16)
            for k in range(FK):
                sp.dma_start(rows[B1 + k:NL:PER_LAYER, :], a["L0_attn_b1"][:, k * P:(k + 1) * P]).then_inc(s["rows_in"], 16)
            for n, name in ((LNL_W, "L0_attn_lnl_w"), (LNL_B, "L0_attn_lnl_b"), (BIN, "L0_attn_bin")):
                sp.dma_start(rows[n:n + 1, :].rearrange("r (o d) -> r o d", o=2),
                             a[name].rearrange("(r o d) -> r o d", r=1, o=1).to_broadcast([1, 2, D])).then_inc(s["rows_in"], 16)
            sp.dma_start(picked_idx[:, 0:PICKED - 1, 0:JG], iu[P:last, :].rearrange("(k p) j -> p k j", p=P)).then_inc(s["idx_in"], 16)
            sp.dma_start(picked_idx[:, 0:PICKED - 1, JG:JP], ig[P:last, 0:JH].rearrange("(k p) j -> p k j", p=P)).then_inc(s["idx_in"], 16)
            for b in range(2):
                gate_index(b, b, None)
                down_index(b, b, None)
            sp.wait_ge(s["idx_cleared"], 2)
            sp.dma_start(picked_idx[:, PICKED, 0:EXTRA], ig[0:P, JH - EXTRA:JH]).then_inc(s["idx_in"], 16)
            sp.dma_start(picked_idx[0:REST, PICKED - 1, 0:JG], iu[last:INNER, :]).then_inc(s["idx_in"], 16)
            sp.dma_start(picked_idx[0:REST, PICKED - 1, JG:JP], ig[last:INNER, 0:JH]).then_inc(s["idx_in"], 16)
            for half in range(2):
                sp.dma_start(book_in[:, 8 * half:8 * half + 8, :, :],
                             a["L0_ffn_codebook"][half * CB // 2:(half + 1) * CB // 2, :].rearrange("(h k p) e -> p h k e", k=LT, p=P)
                             ).then_inc(s["book_in"], 16)
            for k in range(PICKED + 1):
                sp.wait_ge(s["parts_kept"], k + 1)
                sp.dma_start(parts[k].rearrange("m j p -> j m p"), parts_t[:, k, :, :]).then_inc(s["parts_out"], 16)
            sp.wait_ge(s["parts_out"], 16 * (PICKED + 1))
            sp.wait_ge(s["last_normed"], NC)
            for slot in range(EXTRA // 4):
                src = parts[PICKED:PICKED + 1, :, 4 * slot:4 * slot + 4, :].rearrange("o m j p -> o m (j p)").to_broadcast([P, 2, 4 * P])
                sp.dma_start(bc[slot % 4][:, :, :], src).then_inc(s[f"bc_in{slot % 4}"], 16)
            with sp.Fori(0, FULL // 2 - 1) as i:
                for b in range(2):
                    turned = TURN_DOWN[b] + 5
                    spread_parts(2 * i + b, range(4))
                    gate_index(b, 2 * i + 2 + b, i + 1)
                    spread_parts(2 * i + b, range(4, turned))
                    down_index(b, 2 * i + 2 + b, i + 1)
                    spread_parts(2 * i + b, range(turned, QUADS))
            spread_parts(PICKED - 2, range(4))
            sp.wait_ge(s["gate_in0"], (FULL // 2) * (16 * JH))
            sp.dma_start(idx_gate[0][0:REST, :], ig[last:INNER, JH:JG]).then_inc(s["gate_index_in0"], 16)
            spread_parts(PICKED - 2, range(4, TURN_DOWN[0] + 5))
            sp.wait_ge(s["down_in0"], (FULL // 2) * (16 * KT * JD))
            sp.dma_start(idx_down[0][:, :, 0:REST // CS], idn[:, :, FULL * JD:]).then_inc(s["down_index_in0"], 16)
            spread_parts(PICKED - 2, range(TURN_DOWN[0] + 5, QUADS))
            spread_parts(PICKED - 1, range(QUADS))
            for t in range(NT):
                sp.wait_ge(s["out_normed"], t + 1)
                sp.dma_start(y_out[:, t, :], x[:, t, :]).then_inc(s["stored"], 16)
            sp.wait_ge(s["stored"], 16 * NT)

        @block.gpsimd
        def _(pool):
            pool.memset(ident[:, :], 0.0).then_inc(s["consts_made"], 1)
            pool.memset(perm[:, :], 0.0).then_inc(s["consts_made"], 1)
            pool.memset(dup_ident[:, :], 0.0).then_inc(s["consts_made"], 1)
            pool.wait_ge(s["consts_made"], 3)
            pool.affine_select(out=ident[:, :], in_=ident[:, :], compare_op=ALU.not_equal, fill=1.0, base=0,
                               pattern=[[-1, P]], channel_multiplier=1).then_inc(s["masks_made"], 1)
            for base, m in ((-D, perm), (D, perm), (0, dup_ident), (-D, dup_ident)):
                if base == D or (base == -D and m is dup_ident):
                    pool.wait_ge(s["masks_made"], 2 if m is perm else 4)
                pool.affine_select(out=m[:, :], in_=m[:, :], compare_op=ALU.not_equal, fill=1.0, base=base,
                                   pattern=[[-1, m.shape[1]]], channel_multiplier=1).then_inc(s["masks_made"], 1)
            pool.memset(adder_in[:, :], 0.0).then_inc(s["consts_made"], 1)
            pool.wait_ge(s["consts_made"], 4)
            block8 = adder_in[:, P - CS:P]
            pool.memset(block8, 1.0).then_inc(s["consts_made"], 1)
            pool.iota(iota_low[:, :], pattern=[[P, LT]], base=0, channel_multiplier=1).then_inc(s["iotas_made"], 1)
            pool.iota(iota_m[:, :], pattern=[[0, 1]], base=0, channel_multiplier=1).then_inc(s["iotas_made"], 1)
            pool.wait_ge(s["consts_made"], 5)
            pool.affine_select(out=block8, in_=block8, compare_op=ALU.is_ge, fill=0.0, base=0,
                               pattern=[[-HIGH, CS]], channel_multiplier=1).then_inc(s["masks_made"], 1)
            pool.wait_ge(s["masks_made"], 6)
            pool.affine_select(out=block8, in_=block8, compare_op=ALU.is_ge, fill=0.0, base=HIGH - 1,
                               pattern=[[HIGH, CS]], channel_multiplier=-1).then_inc(s["masks_made"], 1)

            def gather(dst, idx, sm):
                pool.indirect_dma_start(dst, None, a["L0_ffn_codebook"],
                                        bass.IndirectOffsetOnAxis(ap=idx, axis=0)).then_inc(sm, 16)

            def gather_gate(b, n):
                for j in range(JH):
                    gather(stage_gate[b][0:n, j * CS:(j + 1) * CS], idx_gate[b][0:n, j:j + 1], s[f"gate_in{b}"])

            def gather_down(b, jd):
                for q in range(KT):
                    for j in range(jd):
                        gather(stage_down[b][:, q, j * CS:(j + 1) * CS], idx_down[b][:, q, j:j + 1], s[f"down_in{b}"])

            def may_gather(index_in, arrived, turned):
                pool.wait_ge(s[index_in], arrived)
                pool.wait_ge(s["turned_stage"], turned)
                pool.sem_inc(s["stage_claimed"], 1)

            pool.wait_ge(s["idx_more_in"], 32)
            for j in range(JE):
                gather(stage_more[:, j * CS:(j + 1) * CS], idx_more[:, j:j + 1], s["more_in"])
            with pool.Fori(0, FULL // 2) as i:
                for b in range(2):
                    k = 2 * i + b
                    k = 2 * i + b
                    may_gather(f"gate_index_in{b}", i * 16 + 16, 2 * k - 3 + AHEAD)
                    gather_gate(b, P)
                    may_gather(f"down_index_in{b}", i * 16 + 16, 2 * k - 2 + AHEAD)
                    gather_down(b, JD)
            may_gather("gate_index_in0", (FULL // 2) * 16 + 16, 2 * FULL - 3 + AHEAD)
            gather_gate(0, REST)
            may_gather("down_index_in0", (FULL // 2) * 16 + 16, 2 * FULL - 2 + AHEAD)
            gather_down(0, REST // CS)

        @block.scalar
        def _(act):
            def load_x(c):
                act.dma_start(x[:, c * TPC:(c + 1) * TPC, :], x_in[:, c * TPC:(c + 1) * TPC, :]).then_inc(s[f"x_in{c}"], 16)

            load_x(0)
            act.dma_start(win_in[:, :], a["L0_attn_Win"]).then_inc(s["w_in"], 16)
            act.dma_start(w1_in[:, :, :], a["L0_attn_W1"].rearrange("l (k p) d -> p (l k) d", p=P)).then_inc(s["w_in"], 16)
            act.dma_start(w2_in[:, :, :], a["L0_attn_W2"].rearrange("l d f -> d l f")).then_inc(s["w_in"], 16)
            act.dma_start(wout_in[:, :, :], a["L0_attn_Wout"].rearrange("(k p) d -> p k d", p=P)).then_inc(s["w_in"], 16)
            act.dma_start(bout_row[:, :], a["L0_attn_bout"].rearrange("(o v) -> o v", o=1)).then_inc(s["bout_in"], 16)
            for c in range(1, NC):
                load_x(c)

            def keep_x(t):
                act.wait_ge(s["turned_x"], t + 1)
                c = t // TPC
                if c >= 2:
                    act.wait_ge(s["h_sum"], c - 1)
                act.activation(xt[:, c % 2 * 2:c % 2 * 2 + 2, :, (t % TPC) * P:(t % TPC + 1) * P],
                               bank[4 + t % 4][:, :].rearrange("p (a b n) -> p a b n", a=2, b=2), ACT.Copy).then_inc(s["x_kept"], 1)

            def keep_h(c):
                act.wait_ge(s["h_sum"], c + 1)
                act.activation(h[:, c * C:(c + 1) * C], bank[c][0:D, :], ACT.Identity, bias=last_cols[0:D, 2:3]).then_inc(s["h_made"], 1)

            for t in range(TPC):
                keep_x(t)
            act.wait_ge(s["q_made"], 1)
            act.activation(small[:, 8, :], small[:, 7, :], ACT.Sqrt).then_inc(s["phase_sqrt"], 1)
            for t in range(TPC, 2 * TPC):
                keep_x(t)
            act.wait_ge(s["mag_made"], 1)
            act.activation(cols[:, :, DECAY], small[:, 9, :], ACT.Tanh).then_inc(s["phase_tanh"], 1)
            act.wait_ge(s["cols_made"], 1)
            keep_h(0)
            for c in range(2, NC):
                for t in range(c * TPC, (c + 1) * TPC):
                    keep_x(t)
                keep_h(c - 1)
            keep_h(NC - 1)

            for k in range(PICKED + 1):
                act.wait_ge(s["parts_turned"], k + 1)
                act.activation(parts_t[:, k, :, :], bank[4 + k % 4][0:JP, 0:2 * P].rearrange("j (m p) -> j m p", m=2),
                               ACT.Copy).then_inc(s["parts_kept"], 1)

            def root(dst, src):
                return act.activation(dst, src, ACT.Abs_reciprocal_sqrt, bias=eps[0:dst.shape[0], :])

            act.sem_inc(s["warmed"], AHEAD)
            act.wait_ge(s["eps_made"], 1)
            with act.Fori(0, L) as l:
                act.wait_ge(s["warmed"], l + AHEAD)
                act.activation(warm[:, :], eps[:, :], ACT.Square).then_inc(s["warmed"], 1)
                for c in range(NC):
                    act.wait_ge(s["centred"], l * 2 * NC + c + 1)
                    act.activation(sq[:, c, :], bank[c][:, :], ACT.Square).then_inc(s["squared"], 1)
                for c in range(NC):
                    act.wait_ge(s["averaged"], l * 2 * NC + c + 1)
                    root(rs[:, c, :], bank[4 + c][:, :]).then_inc(s["rooted"], 1)
                act.wait_ge(s["layer_cols"], l + 1)
                for c in range(NC):
                    act.wait_ge(s["normed"], l * NC + c + 1)
                    act.activation(sq[:, c, :], xn[:, c, :], ACT.Silu, bias=lay[:, LN1_B:LN1_B + 1],
                                   scale=lay[:, LN1_W:LN1_W + 1]).then_inc(s["silu_made"], 1)
                act.wait_ge(s["h_made"], l * NC + NC)
                act.wait_ge(s["w_kept"], 5)
                act.activation(w1t[:, :], w1t_all[:, bass.ds(l, 1), :].rearrange("d o f -> d (o f)"), ACT.Copy).then_inc(s["w_copied"], 1)
                act.activation(w2t[:, :, :].rearrange("p k d -> p (k d)"),
                               w2t_all[:, bass.ds(l, 1), :, :].rearrange("p o k d -> p (o k d)"), ACT.Copy).then_inc(s["w_copied"], 1)
                for c in range(NC):
                    act.wait_ge(s["centred"], l * 2 * NC + NC + c + 1)
                    act.activation(sq[0:D, c, :], bank[4 + c][0:D, :], ACT.Square).then_inc(s["squared"], 1)
                for c in range(NC):
                    act.wait_ge(s["averaged"], l * 2 * NC + NC + c + 1)
                    root(rs[0:D, c, :], bank[c][0:D, :]).then_inc(s["rooted"], 1)
                for c in range(NC):
                    act.wait_ge(s["spread"], l * NC + c + 1)
                    for k in range(FK):
                        last = act.activation(ff[:, c, k, :], bank[4 * k + c][:, :], ACT.Silu, bias=lay[:, B1P + k:B1P + k + 1])
                    last.then_inc(s["ff_made"], 1)
            for c in range(NC):
                act.wait_ge(s["centred"], L * 2 * NC + c + 1)
                act.activation(sq[0:D, c, :], bank[c][0:D, :], ACT.Square).then_inc(s["squared"], 1)
            for c in range(NC):
                act.wait_ge(s["averaged"], L * 2 * NC + c + 1)
                root(rs[0:D, c, :], bank[4 + c][0:D, :]).then_inc(s["rooted"], 1)

            def keep_x1(t):
                act.wait_ge(s["x1_turned"], t + 1)
                act.activation(x1t_hi[:, :, t * P:(t + 1) * P], bank[4 + t % 4][:, :].rearrange("p (k n) -> p k n", k=KT),
                               ACT.Copy).then_inc(s["x1_hi"], 1)

            def normalize(t, shifted, signal):
                act.wait_ge(s["shift_made"], shifted)
                act.activation(x[:, t, :], x[:, t, :], ACT.Identity, bias=shift[:, t:t + 1], scale=rstd[:, t:t + 1]).then_inc(s[signal], 1)

            for t in range(NT + 2):
                if t < NT:
                    act.wait_ge(s["aggregated"], t + 1)
                    root(rstd[:, t:t + 1], mv[:, t, 1:2]).then_inc(s["rstd_made"], 1)
                if 1 <= t <= NT:
                    normalize(t - 1, t, "x1_made")
                if t >= 2:
                    keep_x1(t - 2)

            def keep_picked(b, n, g):
                act.wait_ge(s["summed"], quads_before(n, 4 * g + 4))
                w, q = (wu[b], g) if g < KT else (wg[b], g - KT)
                act.activation(w[:, :, q, :], bank[3][:, 0:2 * P].rearrange("p (m n) -> p m n", m=2), ACT.Copy).then_inc(s["picked_kept"], 1)

            def gate_hi(b, k, n):
                act.wait_ge(s["turned_stage"], 2 * k + 1 + AHEAD)
                act.activation(wg[b][:, 0, 2:KT, 0:n], bank[0][:, 0:2 * P].rearrange("p (k n) -> p k n", k=2)[:, :, 0:n],
                               ACT.Copy).then_inc(s["w_hi"], 1)

            def down_hi(b, k, n):
                act.wait_ge(s["turned_stage"], 2 * k + 2 + AHEAD)
                act.activation(wd[b][0:n, 0, :], bank[2][0:n, :], ACT.Copy).then_inc(s["w_hi"], 1)

            def silu(b, k, n, c):
                act.wait_ge(s["gate_made"], NC * k + c + 1)
                act.wait_ge(s["act_lo_made"], NC * k + c - 1 + AHEAD)
                act.activation(prod[0:n, c % 2, :], bank[0][0:n, :], ACT.Silu).then_inc(s["gate_silu"], 1)

            def product_hi(b, k, n, c):
                act.wait_ge(s["product"], NC * k + c + 1 + AHEAD)
                act.activation(act_hi[0:n, b, c * C:(c + 1) * C], prod[0:n, c % 2, :], ACT.Copy).then_inc(s["act_hi_made"], 1)

            act.sem_inc(s["picked_kept"], AHEAD - 1)
            act.sem_inc(s["gate_silu"], AHEAD)
            act.wait_ge(s["more_turned"], 1)
            act.activation(wu[0][:, 0, :, :], bank[1][:, :].rearrange("p (k n) -> p k n", k=KT), ACT.Copy).then_inc(s["more_hi"], 1)
            act.wait_ge(s["more_turned"], 2)
            act.activation(wg[0][:, 0, 0, :], bank[2][:, 0:P], ACT.Copy).then_inc(s["more_hi"], 1)
            act.wait_ge(s["summed"], EXTRA // 4)
            act.activation(wg[0][:, :, 1, :], bank[3][:, 0:2 * P].rearrange("p (m n) -> p m n", m=2), ACT.Copy).then_inc(s["picked_kept"], 1)
            with act.Fori(0, FULL // 2) as i:
                for b in range(2):
                    k = 2 * i + b
                    gate_hi(b, k, P)
                    for slot in range(QUADS):
                        if slot % 4 == 0 and slot:
                            keep_picked(1 - b, k, slot // 4 - 1)
                        c, share = divmod(slot, SHARES[b])
                        if c < NC and share == SHARES[b] // 2:
                            silu(b, k, P, c)
                        if 1 <= c <= NC and share == 1:
                            product_hi(b, k, P, c - 1)
                        if slot == TURN_DOWN[b]:
                            down_hi(b, k, P)
                    keep_picked(1 - b, k, GROUPS - 1)
                    if NC * SHARES[b] == QUADS:
                        product_hi(b, k, P, NC - 1)
            def out_roots(c):
                act.wait_ge(s["aggregated"], NT + (c + 1) * TPC)
                tiles = slice(c * TPC, (c + 1) * TPC)
                root(rstd[:, tiles], mv[:, tiles, 1:2].rearrange("p t o -> p (t o)")).then_inc(s["rstd_made"], 1)

            gate_hi(0, FULL, REST)
            for c in range(NC):
                silu(0, FULL, REST, c)
                product_hi(0, FULL, REST, c)
                if c == 0:
                    down_hi(0, FULL, REST)
                if c == NC - 2:
                    out_roots(0)
            for c in range(NC):
                if c:
                    out_roots(c)
                for t in range(c * TPC, (c + 1) * TPC):
                    normalize(t, NT + c + 1, "out_normed")

        @block.tensor
        def _(pe):
            def mm(dst, lhs, rhs, start=True, stop=True):
                return pe.matmul(dst, lhs, rhs, start=start, stop=stop)

            pe.sem_inc(s["turned_stage"], AHEAD)
            pe.wait_ge(s["masks_made"], 1)
            pe.wait_ge(s["rows_in"], 16 * ROW_DMAS)
            pe.transpose(bank[0][:, 0:ROWS], rows[:, :], ident[0:ROWS, 0:ROWS]).then_inc(s["turned_w"], 1)

            def turn_x(t):
                if t % TPC == 0:
                    pe.wait_ge(s[f"x_in{t // TPC}"], 16)
                if t >= 4:
                    pe.wait_ge(s["x_kept"], t - 3)
                for k in range(KT):
                    last = pe.transpose(bank[4 + t % 4][:, k * P:(k + 1) * P], x[:, t, k * P:(k + 1) * P], ident[:, :])
                last.then_inc(s["turned_x"], 1)

            def h_in(c):
                pe.wait_ge(s["x_kept"], (c + 1) * TPC)
                if c == 0:
                    pe.wait_ge(s["w_kept"], 5)
                    pe.wait_ge(s["b1_made"], 1)
                for k in range(KT):
                    last = mm(bank[c][0:D, :], wint[:, k, :], xt[:, c % 2 * 2 + k // 2, k % 2, :], k == 0, k == KT - 1)
                last.then_inc(s["h_sum"], 1)

            for t in range(TPC):
                turn_x(t)
            pe.wait_ge(s["w_in"], 64)
            for half in range(2):
                for n in range(4):
                    m = half * 4 + n
                    last = pe.transpose(bank[1 + half][0:D, n * P:(n + 1) * P], w1_in[:, m, :], ident[:, :])
                last.then_inc(s["turned_w"], 1)
            for m in range(L * FK):
                last = pe.transpose(bank[3][:, m * D:(m + 1) * D], w2_in[:, m // FK, (m % FK) * P:(m % FK + 1) * P], ident[0:D, 0:D])
            last.then_inc(s["turned_w"], 1)
            pe.wait_ge(s["w_kept"], 2)
            for k in range(KT):
                last = pe.transpose(bank[1][:, k * D:(k + 1) * D], win_in[:, k * P:(k + 1) * P], ident[0:D, 0:D])
            last.then_inc(s["turned_w"], 1)
            for k in range(KT):
                last = pe.transpose(bank[2][0:D, k * P:(k + 1) * P], wout_in[:, k, :], ident[:, :])
            last.then_inc(s["turned_w"], 1)
            for t in range(TPC, 2 * TPC):
                turn_x(t)
            pe.wait_ge(s["cols_made"], 1)
            pe.wait_ge(s["w_kept"], 5)
            for m in range(L * FK):
                last = mm(bank[0][:, m:m + 1], w1t_all[:, m // FK, (m % FK) * P:(m % FK + 1) * P], cols[0:D, m // FK, LN2_B:LN2_B + 1])
            last.then_inc(s["b1_sum"], 1)
            mm(bank[3][0:1, :], last_cols[0:D, 1:2], woutt[0:D, :]).then_inc(s["bout_sum"], 1)
            h_in(0)
            for c in range(2, NC):
                for t in range(c * TPC, (c + 1) * TPC):
                    turn_x(t)
                h_in(c - 1)
            pe.wait_ge(s["bout_made"], 1)
            h_in(NC - 1)
            pe.wait_ge(s["idx_split"], 1)
            for k in range(PICKED + 1):
                if k < 4:
                    pe.wait_ge(s["x_kept"], NT)
                else:
                    pe.wait_ge(s["parts_kept"], k - 3)
                for m, part in enumerate((low_f, high_f)):
                    last = pe.transpose(bank[4 + k % 4][0:JP, m * P:(m + 1) * P], part[:, k * JP:(k + 1) * JP], ident[:, :])
                last.then_inc(s["parts_turned"], 1)
            pe.wait_ge(s["parts_kept"], PICKED + 1)

            pe.wait_ge(s["means_made"], 3)
            pe.wait_ge(s["h_made"], NC)
            with pe.Fori(0, L) as l:
                for c in range(NC):
                    pe.wait_ge(s["h_made"], l * NC + c + 1)
                    mm(bank[c][:, :], centre[:, :], h[:, c * C:(c + 1) * C]).then_inc(s["centred"], 1)
                for c in range(NC):
                    pe.wait_ge(s["squared"], l * 2 * NC + c + 1)
                    mm(bank[4 + c][:, :], mean_p[:, :], sq[:, c, :]).then_inc(s["averaged"], 1)
                pe.wait_ge(s["layer_cols"], l + 1)
                for c in range(NC):
                    if c < NC - 1:
                        pe.wait_ge(s["scanned"], l * NC + c + 1)
                        mm(bank[4 + c][:, 0:1], turn[:, :], g[:, c, C - 1:C]).then_inc(s["rotated"], 1)
                    pe.wait_ge(s["damped"], l * NC + c + 1)
                    mm(bank[c][0:D, :], scale_add[:, :], xn[:, c, :]).then_inc(s["mixed"], 1)
                for c in range(NC):
                    pe.wait_ge(s["h_mid"], l * NC + c + 1)
                    mm(bank[4 + c][:, :], centre[:, :], h[:, c * C:(c + 1) * C]).then_inc(s["centred"], 1)
                for c in range(NC):
                    pe.wait_ge(s["squared"], l * 2 * NC + NC + c + 1)
                    mm(bank[c][:, :], mean_d[:, :], sq[0:D, c, :]).then_inc(s["averaged"], 1)
                pe.wait_ge(s["w_copied"], 2 * l + 2)
                for c in range(NC):
                    pe.wait_ge(s["normed2"], l * NC + c + 1)
                    for k in range(FK):
                        last = mm(bank[4 * k + c][:, :], w1t[:, k * P:(k + 1) * P], g[0:D, c, :])
                    last.then_inc(s["spread"], 1)
                for c in range(NC):
                    pe.wait_ge(s["ff_made"], l * NC + c + 1)
                    for k in range(FK):
                        last = mm(bank[c][0:D, :], w2t[:, k, :], ff[:, c, k, :], k == 0, k == FK - 1)
                    last.then_inc(s["ff_back"], 1)
            for c in range(NC):
                pe.wait_ge(s["h_made"], L * NC + c + 1)
                mm(bank[c][:, :], centre[:, :], h[:, c * C:(c + 1) * C]).then_inc(s["centred"], 1)
            for c in range(NC):
                pe.wait_ge(s["squared"], L * 2 * NC + c + 1)
                mm(bank[4 + c][:, :], mean_d[:, :], sq[0:D, c, :]).then_inc(s["averaged"], 1)

            def turn_x1(t):
                pe.wait_ge(s["x1_made"], t + 1)
                if t >= 4:
                    pe.wait_ge(s["x1_lo"], t - 3)
                for k in range(KT):
                    last = pe.transpose(bank[4 + t % 4][:, k * P:(k + 1) * P], x[:, t, k * P:(k + 1) * P], ident[:, :])
                last.then_inc(s["x1_turned"], 1)

            pe.wait_ge(s["last_normed"], NC)
            for t in range(NT + 3):
                if t < NT:
                    if t >= 4:
                        pe.wait_ge(s["x_added"], t - 3)
                    mm(bank[t % 4][:, :], hn[:, t * P:(t + 1) * P], woutt[:, :]).then_inc(s["attn_out"], 1)
                if t >= 3:
                    turn_x1(t - 3)

            def exact3(dst, w, v, start, stop):
                mm(dst, w[0], v[0], start, False)
                mm(dst, w[0], v[1], False, False)
                return mm(dst, w[1], v[0], False, stop)

            def candidates(n, slot):
                done = quads_before(n, slot)
                pe.wait_ge(s["one_hot_made"], done + 1)
                if n is not None or slot >= 2:
                    pe.wait_ge(s["chosen_made"], done - 1)
                for m in range(2):
                    for q in range(LT):
                        last = mm(bank[4 + 2 * (slot % 2) + m][:, :], book[m][:, q, :], one_hot[slot % 2][:, q, :], q == 0, q == LT - 1)
                last.then_inc(s["candidates"], 1)

            def add_up(n, slot):
                pe.wait_ge(s["chosen_made"], quads_before(n, slot) + 1)
                if n is not None and slot % 4 == 0:
                    pe.wait_ge(s["picked_kept"], n * GROUPS + slot // 4 + AHEAD)
                for jj in range(4):
                    j = slot % 4 * 4 + jj
                    last = mm(bank[3][:, 0:2 * P].rearrange("p (m n) -> p m n", m=2), adder[:, P - CS - CS * j:2 * P - CS - CS * j],
                              chosen[slot % 2][:, :, jj * P:(jj + 1) * P], j == 0, j == JD - 1)
                last.then_inc(s["summed"], 1)

            def turn_gate(b, i, k, n):
                pe.wait_ge(s["gate_silu"], NC * k + AHEAD)
                pe.wait_ge(s[f"gate_in{b}"], i * (16 * JH) + 16 * JH)
                for q in range(2):
                    last = pe.transpose(bank[0][:, q * P:q * P + n], stage_gate[b][0:n, q * P:(q + 1) * P], ident[0:n, 0:n])
                last.then_inc(s["turned_stage"], 1)

            def turn_down(b, i, n):
                if b == 0:
                    pe.wait_ge(s["down_added"], NT * i + AHEAD)
                pe.wait_ge(s[f"down_in{b}"], i * (16 * KT * JD) + 16 * KT * (n // CS))
                for q in range(KT):
                    last = pe.transpose(bank[2][0:n, q * P:(q + 1) * P], stage_down[b][:, q, 0:n], ident[:, :])
                last.then_inc(s["turned_stage"], 1)

            def hidden(b, k, n, c, share, shares):
                tok = slice(c * C, (c + 1) * C)
                count = 2 * KT * 3
                for m in range(share * count // shares, (share + 1) * count // shares):
                    is_up, (q, part) = m // (KT * 3), divmod(m % (KT * 3), 3)
                    first, last = m % (KT * 3) == 0, m % (KT * 3) == KT * 3 - 1
                    w, dst, made, read = (wu[b], 1, "up_made", "product") if is_up else (wg[b], 0, "gate_made", "gate_silu")
                    if m == 0 and c == 0:
                        pe.wait_ge(s["picked_kept"], k * GROUPS + AHEAD)
                        pe.wait_ge(s["w_hi"], 2 * k + 1)
                        pe.wait_ge(s["w_lo"], 2 * k + 1)
                    if first:
                        pe.wait_ge(s[read], NC * k + c + AHEAD)
                    done = mm(bank[dst][0:n, :], w[:, part // 2, q, 0:n], (x1t_hi, x1t_lo, x1t_hi)[part][:, q, tok], first, last)
                    if last:
                        done.then_inc(s[made], 1)

            def down(i, k, n, tiles, t, banks):
                if t == 0:
                    pe.wait_ge(s["w_hi"], 2 * k + 2)
                    pe.wait_ge(s["w_lo"], 2 * k + 2)
                if t % TPC == 0:
                    pe.wait_ge(s["act_hi_made"], NC * k + t // TPC + 1)
                    pe.wait_ge(s["act_lo_made"], NC * k + t // TPC + 1 + AHEAD)
                if t >= len(banks):
                    pe.wait_ge(s["down_added"], NT * i + t + 1 - len(banks) + AHEAD)
                tok = slice(t * P, (t + 1) * P)
                for b in range(tiles):
                    last = exact3(bank[banks[t % len(banks)]][:, :], (act_hi[0:n, b, tok], act_lo[0:n, b, tok]),
                                  (wd[b][0:n, 0, :], wd[b][0:n, 1, :]), b == 0, b == tiles - 1)
                last.then_inc(s["down_made"], 1)

            pe.wait_ge(s["x_added"], NT)
            pe.wait_ge(s["more_in"], 16 * JE)
            for dst, first, count in ((1, 0, KT), (2, KT, 1)):
                for q in range(count):
                    last = pe.transpose(bank[dst][:, q * P:(q + 1) * P], stage_more[:, (first + q) * P:(first + q + 1) * P], ident[:, :])
                last.then_inc(s["more_turned"], 1)
            for slot in range(EXTRA // 4 + 1):
                if slot < 2:
                    pe.wait_ge(s["x1_lo"], NT - 2 + 2 * slot)
                if slot < EXTRA // 4:
                    candidates(None, slot)
                if slot:
                    add_up(None, slot - 1)
            pe.wait_ge(s["more_hi"], 2)
            pe.wait_ge(s["more_lo"], 2)
            with pe.Fori(0, FULL // 2) as i:
                for b in range(2):
                    k = 2 * i + b
                    for slot in range(QUADS + 1):
                        if slot < QUADS:
                            candidates(k, slot)
                        if slot == 0:
                            turn_gate(b, i, k, P)
                        if 0 < slot < QUADS:
                            add_up(k, slot - 1)
                        if 1 <= slot <= NC * SHARES[b]:
                            c, share = divmod(slot - 1, SHARES[b])
                            hidden(b, k, P, c, share, SHARES[b])
                        if slot == TURN_DOWN[b]:
                            turn_down(b, i, P)
                        if b and 0 <= slot - FIRST_DOWN < NT:
                            down(i, k, P, 2, slot - FIRST_DOWN, (2,))
                        if slot == QUADS:
                            add_up(k, slot - 1)
            turn_gate(0, FULL // 2, FULL, REST)
            for c in range(NC + 1):
                if c < NC:
                    hidden(0, FULL, REST, c, 0, 1)
                if c == 0:
                    turn_down(0, FULL // 2, REST)
                else:
                    for t in range((c - 1) * TPC, c * TPC):
                        down(FULL // 2, FULL, REST, 1, t, (2, 4, 5, 6))

        @block.vector
        def _(v):
            chained = [0]

            def link(ins):
                chained[0] += 1
                ins.then_inc(s["link"], 1)
                v.wait_ge(s["link"], chained[0])

            def tt(o, x0, x1, op):
                return v.tensor_tensor(o, x0, x1, op)

            v.sem_inc(s["act_lo_made"], AHEAD)
            v.sem_inc(s["product"], AHEAD)
            v.sem_inc(s["down_added"], AHEAD)
            v.memset(picked_idx[REST:P, PICKED - 1, :], 0).then_inc(s["idx_cleared"], 1)
            v.memset(picked_idx[:, PICKED, EXTRA:JP], 0).then_inc(s["idx_cleared"], 1)
            v.memset(eps[:, :], EPS).then_inc(s["eps_made"], 1)
            v.memset(mean_p[:, :], 1.0 / P).then_inc(s["means_made"], 1)
            v.memset(mean_d[:, :], 1.0 / D).then_inc(s["means_made"], 1)
            v.memset(hn[D:D + 1, :], 1.0)
            v.memset(sgn[0:D, :], 1.0)
            v.memset(sgn[D:P, :], -1.0)
            v.memset(tab[0:D, :, 0:1], 1.0)
            v.memset(tab[D:P, :, 0:1], 0.0)
            v.memset(tabq[0:D, :, 0:1], 0.0)
            link(v.memset(tabq[D:P, :, 0:1], 1.0))
            v.wait_ge(s["masks_made"], 5)
            v.tensor_scalar(centre[:, 0:D], ident[0:D, 0:D], -1.0 / D, None, ALU.add)
            v.tensor_scalar(centre[:, D:P], ident[0:D, 0:D], -1.0 / D, None, ALU.add).then_inc(s["means_made"], 1)
            v.wait_ge(s["turned_w"], 1)
            v.tensor_copy(cols[:, :, 0:PER_LAYER], bank[0][:, 0:NL].rearrange("p (l k) -> p l k", l=L))
            v.tensor_copy(last_cols[:, :], bank[0][:, NL:ROWS]).then_inc(s["cols_made"], 1)
            v.wait_ge(s["cols_made"], 1)
            re, im = cols[:, :, PHZ_RE], cols[:, :, PHZ_IM]
            S = [small[:, n, :] for n in range(12)]
            v.scalar_tensor_tensor(S[0], re, -1.0, re, ALU.mult, ALU.max)
            link(v.scalar_tensor_tensor(S[1], im, -1.0, im, ALU.mult, ALU.max))
            link(tt(S[2], S[0], S[1], ALU.max))
            v.tensor_scalar(S[0], S[2], TINY, None, ALU.max)
            v.tensor_scalar(S[3], S[2], TINY, None, ALU.is_ge)
            link(v.tensor_scalar(S[4], S[2], TINY, None, ALU.is_lt))
            link(v.reciprocal(S[1], S[0]))
            v.tensor_tensor(S[5], re, S[1], ALU.mult)
            link(v.tensor_tensor(S[6], im, S[1], ALU.mult))
            link(tt(S[0], S[5], S[3], ALU.mult))
            v.tensor_tensor(S[6], S[6], S[3], ALU.mult)
            link(tt(S[5], S[0], S[4], ALU.add))
            v.tensor_tensor(S[0], S[5], S[5], ALU.mult)
            link(tt(S[1], S[6], S[6], ALU.mult))
            tt(S[7], S[0], S[1], ALU.add).then_inc(s["q_made"], 1)

            v.wait_ge(s["idx_in"], 80)
            link(v.tensor_scalar(low_i, high_i, LOW - 1, None, ALU.bitwise_and))
            v.tensor_copy(low_f, low_i)
            link(v.tensor_scalar(high_i, high_i, LOW.bit_length() - 1, None, ALU.logical_shift_right))
            v.tensor_copy(high_f, high_i).then_inc(s["idx_split"], 1)

            v.wait_ge(s["turned_w"], 2)
            v.tensor_copy(w1t_all[:, 0:2, :].rearrange("d l f -> d (l f)"), bank[1][0:D, :]).then_inc(s["w_kept"], 1)
            v.wait_ge(s["turned_w"], 3)
            v.tensor_copy(w1t_all[:, 2:4, :].rearrange("d l f -> d (l f)"), bank[2][0:D, :]).then_inc(s["w_kept"], 1)
            v.wait_ge(s["turned_w"], 4)
            v.tensor_copy(w2t_all[:, :, :, :].rearrange("p l k d -> p (l k d)"), bank[3][:, :]).then_inc(s["w_kept"], 1)
            v.wait_ge(s["turned_w"], 5)
            v.tensor_copy(wint[:, :, :].rearrange("p k d -> p (k d)"), bank[1][:, 0:KT * D]).then_inc(s["w_kept"], 1)
            v.wait_ge(s["turned_w"], 6)
            v.tensor_copy(woutt[0:D, :], bank[2][0:D, :]).then_inc(s["w_kept"], 1)

            v.wait_ge(s["phase_sqrt"], 1)
            tt(S[9], S[2], S[8], ALU.mult).then_inc(s["mag_made"], 1)
            link(v.reciprocal(S[3], S[8]))

            def unit(k, x0, y0):
                tt(S[0], x0, x0, ALU.mult)
                link(tt(S[1], y0, y0, ALU.mult))
                link(tt(S[4], S[0], S[1], ALU.add))
                link(v.tensor_scalar(S[0], S[4], -0.5, 1.5, ALU.mult, ALU.add))
                tt(cosp[:, :, k], x0, S[0], ALU.mult)
                link(tt(sinp[:, :, k], y0, S[0], ALU.mult))

            tt(S[10], S[5], S[3], ALU.mult)
            link(tt(S[11], S[6], S[3], ALU.mult))
            unit(0, S[10], S[11])
            v.wait_ge(s["b1_sum"], 1)
            v.tensor_tensor(cols[:, :, B1P:B1P + FK], cols[:, :, B1:B1 + FK], bank[0][:, 0:L * FK].rearrange("p (l k) -> p l k", l=L),
                            ALU.add).then_inc(s["b1_made"], 1)
            v.wait_ge(s["bout_sum"], 1)
            v.wait_ge(s["bout_in"], 16)
            tt(woutt[D:D + 1, :], bank[3][0:1, :], bout_row[:, :], ALU.add).then_inc(s["bout_made"], 1)
            for k in range(9):
                w = 1 << k
                cw = cosp[:, :, k:k + 1].to_broadcast([P, L, w])
                sw = sinp[:, :, k:k + 1].to_broadcast([P, L, w])
                old, new = slice(0, w), slice(w, 2 * w)
                ta, tb = tmp[:, :, 0:w], tmp[:, :, C // 2:C // 2 + w]
                tt(ta, tab[:, :, old], cw, ALU.mult)
                link(tt(tb, tabq[:, :, old], sw, ALU.mult))
                link(tt(tab[:, :, new], ta, tb, ALU.subtract))
                if k < 8:
                    tt(ta, tab[:, :, old], sw, ALU.mult)
                    link(tt(tb, tabq[:, :, old], cw, ALU.mult))
                    tt(tabq[:, :, new], ta, tb, ALU.add)
                tt(S[0], cosp[:, :, k], cosp[:, :, k], ALU.mult)
                tt(S[1], sinp[:, :, k], sinp[:, :, k], ALU.mult)
                link(v.scalar_tensor_tensor(S[11], cosp[:, :, k], 2.0, sinp[:, :, k], ALU.mult, ALU.mult))
                link(tt(S[10], S[0], S[1], ALU.subtract))
                unit(k + 1, S[10], S[11])
            sg = sgn[:, 0:1].to_broadcast([P, L])
            v.tensor_copy(cols[:, :, COS_C], cosp[:, :, 9])
            tt(cols[:, :, SIN_C], sinp[:, :, 9], sg, ALU.mult)
            tt(S[0], cols[:, :, LC_RE], tab[:, :, 1], ALU.mult)
            link(tt(S[1], cols[:, :, LC_IM], tabq[:, :, 1], ALU.mult))
            link(tt(S[4], S[0], S[1], ALU.subtract))
            link(tt(cols[:, :, STATE0], S[4], sg, ALU.mult))
            v.wait_ge(s["b1_made"], 1)
            v.wait_ge(s["phase_tanh"], 1)

            with v.Fori(0, L) as l:
                v.wait_ge(s["h_made"], l * NC + NC)
                v.tensor_copy(tab_l[:, :], tab[:, bass.ds(l, 1), :].rearrange("p o c -> p (o c)"))
                v.tensor_copy(lay[:, :], cols[:, bass.ds(l, 1), :].rearrange("p o c -> p (o c)")).then_inc(s["lay_kept"], 1)
                v.wait_ge(s["lay_kept"], l + 1)
                v.tensor_scalar(turn_a[:, :], perm[:, :], lay[:, SIN_C:SIN_C + 1], None, ALU.mult).then_inc(s["turn_begun"], 1)
                v.tensor_scalar(scale_add[:, :], dup_ident[:, :], lay[:, SC_LIN:SC_LIN + 1], None, ALU.mult)
                v.wait_ge(s["turn_begun"], l + 1)
                v.scalar_tensor_tensor(turn[:, :], ident[:, :], lay[:, COS_C:COS_C + 1], turn_a[:, :], ALU.mult, ALU.add
                                       ).then_inc(s["layer_cols"], 1)
                for c in range(NC):
                    v.wait_ge(s["rooted"], l * 2 * NC + c + 1)
                    tt(xn[:, c, :], bank[c][:, :], rs[:, c, :], ALU.mult).then_inc(s["normed"], 1)
                for c in range(NC):
                    v.wait_ge(s["silu_made"], l * NC + c + 1)
                    tt(xn[:, c, :], sq[:, c, :], tab_l[:, :], ALU.mult).then_inc(s["turned_back"], 1)
                    v.wait_ge(s["turned_back"], l * NC + c + 1)
                    if c:
                        v.wait_ge(s["rotated"], l * (NC - 1) + c)
                    state = bank[4 + c - 1][:, 0:1] if c else lay[:, STATE0:STATE0 + 1]
                    v.tensor_tensor_scan(g[:, c, :], lay[:, DECAY:DECAY + 1].to_broadcast([P, C]), xn[:, c, :], state,
                                         ALU.mult, ALU.add).then_inc(s["scanned"], 1)
                    v.wait_ge(s["scanned"], l * NC + c + 1)
                    tt(xn[:, c, :], g[:, c, :], tab_l[:, :], ALU.mult).then_inc(s["damped"], 1)
                for c in range(NC):
                    v.wait_ge(s["mixed"], l * NC + c + 1)
                    hc = h[:, c * C:(c + 1) * C]
                    tt(hc, hc, bank[c][0:D, :], ALU.add).then_inc(s["h_mid"], 1)
                for c in range(NC):
                    v.wait_ge(s["rooted"], l * 2 * NC + NC + c + 1)
                    v.scalar_tensor_tensor(g[0:D, c, :], bank[4 + c][0:D, :], lay[0:D, LN2_W:LN2_W + 1], rs[0:D, c, :],
                                           ALU.mult, ALU.mult).then_inc(s["normed2"], 1)
                for c in range(NC):
                    v.wait_ge(s["ff_back"], l * NC + c + 1)
                    hc = h[:, c * C:(c + 1) * C]
                    v.scalar_tensor_tensor(hc, bank[c][0:D, :], lay[0:D, B2:B2 + 1], hc, ALU.add, ALU.add).then_inc(s["h_made"], 1)
            v.wait_ge(s["iotas_made"], 2)
            v.wait_ge(s["masks_made"], 7)
            v.wait_ge(s["book_in"], 32)
            v.tensor_copy(low_of[:, :], iota_low[:, :])
            link(v.tensor_scalar(iota_m[:, :], iota_m[:, :], HIGH - 1, None, ALU.bitwise_and))
            v.tensor_copy(high_of[:, :], iota_m[:, :])
            v.tensor_copy(adder[:, :], adder_in[:, :])
            for q in range(LT):
                link(v.tensor_copy(book[0][:, q, :].rearrange("p (e h) -> p h e", e=CS), book_in[:, :, q, :]))
                tt(book[1][:, q, :].rearrange("p (e h) -> p h e", e=CS), book_in[:, :, q, :],
                   book[0][:, q, :].rearrange("p (e h) -> p h e", e=CS).bitcast(F32), ALU.subtract).then_inc(s["book_made"], 1)
            for c in range(NC):
                v.wait_ge(s["rooted"], L * 2 * NC + c + 1)
                v.scalar_tensor_tensor(hn[0:D, c * C:(c + 1) * C], bank[c][0:D, :], last_cols[0:D, 0:1], rs[0:D, c, :],
                                       ALU.mult, ALU.mult).then_inc(s["last_normed"], 1)

            def measure(t, n):
                v.bn_stats(stats[:, t, :], x[:, t, :]).then_inc(s["stats_made"], 1)
                v.wait_ge(s["stats_made"], n + 1)
                v.bn_aggr(mv[:, t, :], stats[:, t, :]).then_inc(s["aggregated"], 1)

            def make_shift(first, n, roots):
                v.wait_ge(s["rstd_made"], roots)
                tiles = slice(first, first + n)
                v.scalar_tensor_tensor(shift[:, tiles], mv[:, tiles, 0:1].rearrange("p t o -> p (t o)"), -1.0, rstd[:, tiles],
                                       ALU.mult, ALU.mult).then_inc(s["shift_made"], 1)

            def keep_lo(t):
                v.wait_ge(s["x1_hi"], t + 1)
                tt(x1t_lo[:, :, t * P:(t + 1) * P], bank[4 + t % 4][:, :].rearrange("p (k n) -> p k n", k=KT),
                   x1t_hi[:, :, t * P:(t + 1) * P].bitcast(F32), ALU.subtract).then_inc(s["x1_lo"], 1)

            def one_hots(n, slot):
                v.wait_ge(s[f"bc_in{slot % 4}"], 16 if n is None else n * (16 * QUADS // 4) + 16 * (slot // 4) + 32)
                if n is not None or slot >= 2:
                    v.wait_ge(s["candidates"], quads_before(n, slot) - 1)
                for q in range(LT):
                    last = v.tensor_scalar(one_hot[slot % 2][:, q, :], bc[slot % 4][:, 0, :], low_of[:, q:q + 1], None,
                                           ALU.is_equal)
                last.then_inc(s["one_hot_made"], 1)

            for t in range(NT + 4):
                if t == NT + 1:
                    one_hots(None, 0)
                    one_hots(None, 1)
                if t < NT:
                    v.wait_ge(s["attn_out"], t + 1)
                    tt(x[:, t, :], x[:, t, :], bank[t % 4][:, :], ALU.add).then_inc(s["x_added"], 1)
                    v.wait_ge(s["x_added"], t + 1)
                    measure(t, t)
                if 1 <= t <= NT:
                    make_shift(t - 1, 1, t)
                if t >= 4:
                    keep_lo(t - 4)

            def choose(n, slot):
                v.wait_ge(s["candidates"], quads_before(n, slot) + 1)
                if n is not None or slot >= 2:
                    v.wait_ge(s["summed"], quads_before(n, slot) - 1)
                for m in range(2):
                    last = v.scalar_tensor_tensor(chosen[slot % 2][:, m, :], bc[slot % 4][:, 1, :], high_of[:, 0:1],
                                                  bank[4 + 2 * (slot % 2) + m][:, :], ALU.is_equal, ALU.mult)
                last.then_inc(s["chosen_made"], 1)

            def gate_lo(b, k, n):
                v.wait_ge(s["w_hi"], 2 * k + 1)
                tt(wg[b][:, 1, 2:KT, 0:n], bank[0][:, 0:2 * P].rearrange("p (k n) -> p k n", k=2)[:, :, 0:n],
                   wg[b][:, 0, 2:KT, 0:n].bitcast(F32), ALU.subtract).then_inc(s["w_lo"], 1)

            def down_lo(b, k, n):
                v.wait_ge(s["w_hi"], 2 * k + 2)
                tt(wd[b][0:n, 1, :], bank[2][0:n, :], wd[b][0:n, 0, :].bitcast(F32), ALU.subtract).then_inc(s["w_lo"], 1)

            def product(b, k, n, c):
                v.wait_ge(s["up_made"], NC * k + c + 1)
                v.wait_ge(s["gate_silu"], NC * k + c + 1 + AHEAD)
                pc = prod[0:n, c % 2, :]
                tt(pc, pc, bank[1][0:n, :], ALU.mult).then_inc(s["product"], 1)

            def product_lo(b, k, n, c):
                v.wait_ge(s["act_hi_made"], NC * k + c + 1)
                tok = slice(c * C, (c + 1) * C)
                tt(act_lo[0:n, b, tok], prod[0:n, c % 2, :], act_hi[0:n, b, tok].bitcast(F32), ALU.subtract).then_inc(s["act_lo_made"], 1)

            def add_down(i, t, banks):
                v.wait_ge(s["down_made"], NT * i + t + 1)
                tt(x[:, t, :], x[:, t, :], bank[banks[t % len(banks)]][:, :], ALU.add).then_inc(s["down_added"], 1)

            choose(None, 0)
            one_hots(None, 2)
            v.wait_ge(s["more_hi"], 1)
            tt(wu[0][:, 1, :, :], bank[1][:, :].rearrange("p (k n) -> p k n", k=KT), wu[0][:, 0, :, :].bitcast(F32), ALU.subtract
               ).then_inc(s["more_lo"], 1)
            choose(None, 1)
            one_hots(None, 3)
            v.wait_ge(s["more_hi"], 2)
            tt(wg[0][:, 1, 0, :], bank[2][:, 0:P], wg[0][:, 0, 0, :].bitcast(F32), ALU.subtract).then_inc(s["more_lo"], 1)
            choose(None, 2)
            choose(None, 3)
            with v.Fori(0, FULL // 2) as i:
                for b in range(2):
                    k = 2 * i + b
                    for slot in range(QUADS):
                        if slot == 0 and b == 0:
                            one_hots(k, 0)
                        if slot == 0 and b:
                            product(0, 2 * i, P, NC - 1)
                        if slot < QUADS - 1:
                            one_hots(k, slot + 1)
                        elif b == 0:
                            one_hots(k + 1, 0)
                        if slot == 0:
                            gate_lo(b, k, P)
                            if b:
                                product_lo(0, 2 * i, P, NC - 1)
                        if slot == TURN_DOWN[b] + 1:
                            down_lo(b, k, P)
                        if b and 0 <= slot - 1 - FIRST_DOWN < NT:
                            add_down(i, slot - 1 - FIRST_DOWN, (2,))
                        choose(k, slot)
                        c, share = divmod(slot, SHARES[b])
                        if 1 <= c <= NC and share == 1:
                            product(b, k, P, c - 1)
                        if 1 <= c <= NC and share == 2:
                            product_lo(b, k, P, c - 1)
                    if b:
                        for t in range(QUADS - 1 - FIRST_DOWN, NT):
                            add_down(i, t, (2,))
            gate_lo(0, FULL, REST)
            for c in range(NC + 1):
                if c < NC:
                    product(0, FULL, REST, c)
                    product_lo(0, FULL, REST, c)
                if c == 0:
                    down_lo(0, FULL, REST)
                else:
                    for t in range((c - 1) * TPC, c * TPC):
                        add_down(FULL // 2, t, (2, 4, 5, 6))
                        v.wait_ge(s["down_added"], NT * (FULL // 2) + t + 1 + AHEAD)
                        measure(t, NT + t)
                if c >= 2:
                    make_shift((c - 2) * TPC, TPC, NT + c - 1)
            make_shift((NC - 1) * TPC, TPC, NT + NC)


_INS = ["L0_attn_x", "L0_attn_Win", "L0_attn_bin", "L0_attn_ln1_w", "L0_attn_ln1_b", "L0_attn_phz_re", "L0_attn_phz_im",
        "L0_attn_lc_re", "L0_attn_lc_im", "L0_attn_sc_lin", "L0_attn_ln2_w", "L0_attn_ln2_b", "L0_attn_W1", "L0_attn_b1",
        "L0_attn_W2", "L0_attn_b2", "L0_attn_lnl_w", "L0_attn_lnl_b", "L0_attn_Wout", "L0_attn_bout", "L0_ffn_codebook",
        "L0_ffn_idx_gate", "L0_ffn_idx_up", "L0_ffn_idx_down"]


def kernel(**inputs):
    import concourse.bacc as bacc
    from concourse.bass_utils import run_bass_kernel_spmd

    nc = bacc.Bacc("TRN2", target_bir_lowering=False, num_devices=1)
    arrays, args = {}, {}
    for name in _INS:
        array = np.ascontiguousarray(inputs[name])
        arrays[f"in_{name}"] = array
        args[name] = nc.dram_tensor(f"in_{name}", array.shape, mybir.dt.from_np(array.dtype), kind="ExternalInput").ap()
    shape = inputs["L0_attn_x"].shape
    out = nc.dram_tensor("out_x", shape, F32, kind="ExternalOutput").ap()
    build(nc, args, out)
    result = run_bass_kernel_spmd(nc, [arrays], core_ids=[0])
    return result.results[0]["out_x"]
```
